# Optimizing a Trainium2 kernel written in Bass

```python
import numpy as np
import jax
import jax.numpy as jnp

def _softmax(x, axis=-1):
    return jax.nn.softmax(x, axis=axis)

def _gelu(x):
    return jax.nn.gelu(x, approximate=True)

def _silu(x):
    return jax.nn.silu(x)

def _sigmoid(x):
    return jax.nn.sigmoid(x)

def _layernorm(x, axis=-1, eps=1e-05):
    m = jnp.mean(x, axis=axis, keepdims=True)
    v = jnp.var(x, axis=axis, keepdims=True)
    return (x - m) / jnp.sqrt(v + eps)

def _scatter_add(tgt, idx, src, axis=0):
    return tgt.at[idx].add(src)

def _segment_sum(src, seg, n):
    return jax.ops.segment_sum(src, seg, n)
kernel_name = 'mk_macaron_d1_jaxref_r8_d9ecf7'

def setup_inputs(seed: int=0):
    np.random.seed(seed)
    _w = jnp.asarray

    def _L0_attn_setup():
        import jax, jax.numpy as jnp
        import numpy as np
        D_OUT = 128
        key = jax.random.key(seed)
        k1, k2 = jax.random.split(key)
        x = jax.random.normal(k1, (4, 256, 128), dtype=jnp.float32)
        W_qkv = jax.random.normal(k2, (128, 3 * D_OUT), dtype=jnp.float32) * 0.02
        return {'x': x, 'W_qkv': W_qkv}
    _L0_attn_in = _L0_attn_setup()

    def _L0_ffn_setup():
        import jax, jax.numpy as jnp
        import numpy as np
        DIM = 128
        DEPTH = 2
        HEADS = 8
        DIM_HEAD = 64
        WINDOW = 64
        INNER = HEADS * DIM_HEAD
        HID = int(DIM * 4 * 2 / 3)
        B, N = (2, 1024)
        QK_SCALE = 8.0

        def shift_token(t):
            t1, t2 = jnp.split(t, 2, axis=-1)
            t2 = jnp.pad(t2, ((0, 0), (1, 0), (0, 0)))[:, :-1]
            return jnp.concatenate([t1, t2], axis=-1)

        def l2norm(t):
            return t / jnp.clip(jnp.linalg.norm(t, axis=-1, keepdims=True), 1e-12)

        def rotate_half(x):
            x1, x2 = jnp.split(x, 2, axis=-1)
            return jnp.concatenate([-x2, x1], axis=-1)

        def rotary_xpos(q, k):
            n = q.shape[-2]
            half_idx = jnp.arange(0, DIM_HEAD, 2, dtype=jnp.float32)
            inv_freq = 1.0 / 10000.0 ** (half_idx / DIM_HEAD)
            t = jnp.arange(n, dtype=jnp.float32)
            freqs = t[:, None] * inv_freq[None, :]
            freqs = jnp.concatenate([freqs, freqs], axis=-1)
            base = (half_idx + 0.4 * DIM_HEAD) / (1.4 * DIM_HEAD)
            power = (t - n // 2) / float(WINDOW // 2)
            scale = base[None, :] ** power[:, None]
            scale = jnp.concatenate([scale, scale], axis=-1)
            cos, sin = (jnp.cos(freqs), jnp.sin(freqs))
            q = q * cos * scale + rotate_half(q) * sin * scale
            k = k * cos / scale + rotate_half(k) * sin / scale
            return (q, k)

        def local_attention(q, k, v):
            b, h, n, d = q.shape
            w = n // WINDOW
            bq = q.reshape(b, h, w, WINDOW, d) * QK_SCALE
            bk = k.reshape(b, h, w, WINDOW, d)
            bv = v.reshape(b, h, w, WINDOW, d)

            def look_around(t):
                p = jnp.pad(t, ((0, 0), (0, 0), (1, 0), (0, 0), (0, 0)))
                return jnp.concatenate([p[:, :, :w], p[:, :, 1:]], axis=3)
            bk, bv = (look_around(bk), look_around(bv))
            bt = jnp.arange(n).reshape(w, WINDOW)
            btp = jnp.pad(bt, ((1, 0), (0, 0)), constant_values=-1)
            btk = jnp.concatenate([btp[:w], btp[1:]], axis=1)
            sim = jnp.einsum('bhwid,bhwjd->bhwij', bq, bk)
            i = bt[:, :, None]
            j = btk[:, None, :]
            mask = (i < j) | (i > j + WINDOW) | (j == -1)
            sim = jnp.where(mask, -jnp.finfo(sim.dtype).max, sim)
            attn = jax.nn.softmax(sim, axis=-1)
            out = jnp.einsum('bhwij,bhwjd->bhwid', attn, bv)
            return out.reshape(b, h, n, d)

        def _layer(x, wqkv, qs, ksc, wo, lg, lb, w1, b1, w2, b2):
            b, n, _ = x.shape
            h = shift_token(x)
            qkv = h @ wqkv
            q, k, v = jnp.split(qkv, 3, axis=-1)
            to_heads = lambda t: t.reshape(b, n, HEADS, DIM_HEAD).transpose(0, 2, 1, 3)
            q, k, v = (to_heads(q), to_heads(k), to_heads(v))
            q = l2norm(q) * qs
            k = l2norm(k) * ksc
            q, k = rotary_xpos(q, k)
            o = local_attention(q, k, v)
            o = o.transpose(0, 2, 1, 3).reshape(b, n, INNER)
            x = x + o @ wo
            h = shift_token(x)
            mu = h.mean(-1, keepdims=True)
            var = h.var(-1, keepdims=True)
            h = (h - mu) / jnp.sqrt(var + 1e-05) * lg + lb
            h = h @ w1 + b1
            a, g = jnp.split(h, 2, axis=-1)
            h = a * jax.nn.gelu(g, approximate=False)
            x = x + h @ w2 + b2
            return x
        key = jax.random.key(seed)
        ks = jax.random.split(key, 6)
        return {'x': jax.random.normal(ks[0], (B, N, DIM), jnp.float32), 'wqkv': jax.random.normal(ks[1], (DEPTH, DIM, 3 * INNER), jnp.float32) * 0.02, 'q_scale': jnp.ones((DEPTH, DIM_HEAD), jnp.float32), 'k_scale': jnp.ones((DEPTH, DIM_HEAD), jnp.float32), 'wo': jax.random.normal(ks[2], (DEPTH, INNER, DIM), jnp.float32) * 0.02, 'ln_g': jnp.ones((DEPTH, DIM), jnp.float32), 'ln_b': jnp.zeros((DEPTH, DIM), jnp.float32), 'w1': jax.random.normal(ks[3], (DEPTH, DIM, 2 * HID), jnp.float32) * 0.02, 'b1': jnp.zeros((DEPTH, 2 * HID), jnp.float32), 'w2': jax.random.normal(ks[4], (DEPTH, HID, DIM), jnp.float32) * 0.02, 'b2': jnp.zeros((DEPTH, DIM), jnp.float32)}
    _L0_ffn_in = _L0_ffn_setup()
    _d = {'L0_attn_x': _L0_attn_in['x'], 'L0_attn_W_qkv': _L0_attn_in['W_qkv'], 'L0_ffn_wqkv': _L0_ffn_in['wqkv'], 'L0_ffn_q_scale': _L0_ffn_in['q_scale'], 'L0_ffn_k_scale': _L0_ffn_in['k_scale'], 'L0_ffn_wo': _L0_ffn_in['wo'], 'L0_ffn_ln_g': _L0_ffn_in['ln_g'], 'L0_ffn_ln_b': _L0_ffn_in['ln_b'], 'L0_ffn_w1': _L0_ffn_in['w1'], 'L0_ffn_b1': _L0_ffn_in['b1'], 'L0_ffn_w2': _L0_ffn_in['w2'], 'L0_ffn_b2': _L0_ffn_in['b2']}
    _x0 = _d['L0_attn_x']
    _d['L0_attn_x'] = jax.random.normal(jax.random.fold_in(jax.random.key(seed), 1), (4, 1024, 128), dtype=_x0.dtype)
    del _x0
    return _d

def reference(L0_attn_x, L0_attn_W_qkv, L0_ffn_wqkv, L0_ffn_q_scale, L0_ffn_k_scale, L0_ffn_wo, L0_ffn_ln_g, L0_ffn_ln_b, L0_ffn_w1, L0_ffn_b1, L0_ffn_w2, L0_ffn_b2):

    def _L0_attn_ref(x, W_qkv):
        import jax, jax.numpy as jnp
        import numpy as np
        D_OUT = 128
        B, N, _ = x.shape
        scale = D_OUT ** 0.5
        qkv = jnp.einsum('bnd,de->bne', x, W_qkv)
        q, k, v = jnp.split(qkv, 3, axis=-1)
        scores = jnp.einsum('bnd,bmd->bnm', q, k) / scale
        causal = jnp.triu(jnp.ones((N, N), dtype=bool), k=1)
        scores = jnp.where(causal, -jnp.inf, scores)
        attn = jax.nn.softmax(scores, axis=-1)
        return jnp.einsum('bnm,bmd->bnd', attn, v)

    def _L0_ffn_ref(x, wqkv, q_scale, k_scale, wo, ln_g, ln_b, w1, b1, w2, b2):
        import jax, jax.numpy as jnp
        import numpy as np
        DIM = 128
        DEPTH = 2
        HEADS = 8
        DIM_HEAD = 64
        WINDOW = 64
        INNER = HEADS * DIM_HEAD
        HID = int(DIM * 4 * 2 / 3)
        B, N = (2, 1024)
        QK_SCALE = 8.0

        def shift_token(t):
            t1, t2 = jnp.split(t, 2, axis=-1)
            t2 = jnp.pad(t2, ((0, 0), (1, 0), (0, 0)))[:, :-1]
            return jnp.concatenate([t1, t2], axis=-1)

        def l2norm(t):
            return t / jnp.clip(jnp.linalg.norm(t, axis=-1, keepdims=True), 1e-12)

        def rotate_half(x):
            x1, x2 = jnp.split(x, 2, axis=-1)
            return jnp.concatenate([-x2, x1], axis=-1)

        def rotary_xpos(q, k):
            n = q.shape[-2]
            half_idx = jnp.arange(0, DIM_HEAD, 2, dtype=jnp.float32)
            inv_freq = 1.0 / 10000.0 ** (half_idx / DIM_HEAD)
            t = jnp.arange(n, dtype=jnp.float32)
            freqs = t[:, None] * inv_freq[None, :]
            freqs = jnp.concatenate([freqs, freqs], axis=-1)
            base = (half_idx + 0.4 * DIM_HEAD) / (1.4 * DIM_HEAD)
            power = (t - n // 2) / float(WINDOW // 2)
            scale = base[None, :] ** power[:, None]
            scale = jnp.concatenate([scale, scale], axis=-1)
            cos, sin = (jnp.cos(freqs), jnp.sin(freqs))
            q = q * cos * scale + rotate_half(q) * sin * scale
            k = k * cos / scale + rotate_half(k) * sin / scale
            return (q, k)

        def local_attention(q, k, v):
            b, h, n, d = q.shape
            w = n // WINDOW
            bq = q.reshape(b, h, w, WINDOW, d) * QK_SCALE
            bk = k.reshape(b, h, w, WINDOW, d)
            bv = v.reshape(b, h, w, WINDOW, d)

            def look_around(t):
                p = jnp.pad(t, ((0, 0), (0, 0), (1, 0), (0, 0), (0, 0)))
                return jnp.concatenate([p[:, :, :w], p[:, :, 1:]], axis=3)
            bk, bv = (look_around(bk), look_around(bv))
            bt = jnp.arange(n).reshape(w, WINDOW)
            btp = jnp.pad(bt, ((1, 0), (0, 0)), constant_values=-1)
            btk = jnp.concatenate([btp[:w], btp[1:]], axis=1)
            sim = jnp.einsum('bhwid,bhwjd->bhwij', bq, bk)
            i = bt[:, :, None]
            j = btk[:, None, :]
            mask = (i < j) | (i > j + WINDOW) | (j == -1)
            sim = jnp.where(mask, -jnp.finfo(sim.dtype).max, sim)
            attn = jax.nn.softmax(sim, axis=-1)
            out = jnp.einsum('bhwij,bhwjd->bhwid', attn, bv)
            return out.reshape(b, h, n, d)

        def _layer(x, wqkv, qs, ksc, wo, lg, lb, w1, b1, w2, b2):
            b, n, _ = x.shape
            h = shift_token(x)
            qkv = h @ wqkv
            q, k, v = jnp.split(qkv, 3, axis=-1)
            to_heads = lambda t: t.reshape(b, n, HEADS, DIM_HEAD).transpose(0, 2, 1, 3)
            q, k, v = (to_heads(q), to_heads(k), to_heads(v))
            q = l2norm(q) * qs
            k = l2norm(k) * ksc
            q, k = rotary_xpos(q, k)
            o = local_attention(q, k, v)
            o = o.transpose(0, 2, 1, 3).reshape(b, n, INNER)
            x = x + o @ wo
            h = shift_token(x)
            mu = h.mean(-1, keepdims=True)
            var = h.var(-1, keepdims=True)
            h = (h - mu) / jnp.sqrt(var + 1e-05) * lg + lb
            h = h @ w1 + b1
            a, g = jnp.split(h, 2, axis=-1)
            h = a * jax.nn.gelu(g, approximate=False)
            x = x + h @ w2 + b2
            return x
        for l in range(DEPTH):
            x = _layer(x, wqkv[l], q_scale[l], k_scale[l], wo[l], ln_g[l], ln_b[l], w1[l], b1[l], w2[l], b2[l])
        return x
    x = L0_attn_x
    x = x + 0.5 * _L0_ffn_ref(_layernorm(x, axis=-1), L0_ffn_wqkv, L0_ffn_q_scale, L0_ffn_k_scale, L0_ffn_wo, L0_ffn_ln_g, L0_ffn_ln_b, L0_ffn_w1, L0_ffn_b1, L0_ffn_w2, L0_ffn_b2)
    x = x + _L0_attn_ref(_layernorm(x, axis=-1), L0_attn_W_qkv)
    x = x + 0.5 * _L0_ffn_ref(_layernorm(x, axis=-1), L0_ffn_wqkv, L0_ffn_q_scale, L0_ffn_k_scale, L0_ffn_wo, L0_ffn_ln_g, L0_ffn_ln_b, L0_ffn_w1, L0_ffn_b1, L0_ffn_w2, L0_ffn_b2)
    return x

_drawn_inputs = setup_inputs


def setup_inputs(seed=0):
    import zlib

    import numpy as np

    out = dict(_drawn_inputs(seed))
    spreads = {'L0_ffn_q_scale': (1.0, 0.6),
     'L0_ffn_k_scale': (1.0, 0.6),
     'L0_ffn_ln_g': (1.0, 0.6),
     'L0_ffn_ln_b': (0.0, 0.8),
     'L0_ffn_b1': (0.0, 0.8),
     'L0_ffn_b2': (0.0, 0.1)}
    factors = {'L0_attn_W_qkv': 3.968,
     'L0_ffn_wqkv': 3.344,
     'L0_ffn_wo': 3.315,
     'L0_ffn_w1': 5.291,
     'L0_ffn_w2': 5.211}
    for name, (base, spread) in spreads.items():
        noise = np.random.default_rng([zlib.crc32(name.encode()), seed]).standard_normal(out[name].shape)
        drawn = base * np.exp(spread * noise) if base else spread * noise
        out[name] = jnp.asarray(drawn.astype(out[name].dtype))
    for name, factor in factors.items():
        out[name] = (out[name] * factor).astype(out[name].dtype)
    return out
```

```python
import numpy as np

import concourse.bass as bass
from concourse import mybir
from contextlib import ExitStack

SEQS, N_TOK, D = 4, 1024, 128
P = 128
TILES = N_TOK // P
GROUP = 4
GROUPS = TILES // GROUP
LAYERS = 2
HEADS, HEAD_D, WINDOW = 8, 64, 64
HALF = HEAD_D // 2
INNER = HEADS * HEAD_D
PAIRS = HEADS // 2
HID = int(D * 4 * 2 / 3)
HID_CHUNKS = [(0, 128), (128, 128), (256, HID - 256)]
N_CHUNKS = len(HID_CHUNKS)
B2_ROW = HID - 256
STEPS = 2 * LAYERS * TILES
LN_EPS = 1e-5
NORM2_MIN = 1e-24
MASKED = -1e30
SCORE_SCALE = float(D) ** -0.5
BANKS = 8
ZEROED = 6


def stage_order():
    order = []
    groups_per_pass = LAYERS * GROUPS

    def open_pass(i):
        for g in range(GROUPS):
            order.append(("input_norm", i * GROUPS + g))

    def local_steps(i):
        first, last = i * LAYERS * TILES, (i + 1) * LAYERS * TILES
        look = 2
        for n in range(first - look, last + 2):
            def add(stage, m):
                if first <= m < last:
                    order.append((stage, m))
            add("transpose_qk", n)
            add("transpose_probs", n - 1)
            add("transpose_x", n + 2)
            add("scores", n)
            add("mix_values", n - 1)
            add("rope_finish", n + 1)
            add("probs_finish", n)
            add("project", n + 2)
            add("attend_out", n - 1)
            m = n - 1
            if first <= m < last and m % GROUP == GROUP - 1:
                order.append(("ff_norm", m // GROUP))
            m = n - 2
            if first <= m < last and m % GROUP == GROUP - 1:
                order.append(("ff_up", m // GROUP))
                order.append(("ff_down", m // GROUP))

    for i in range(2):
        open_pass(i)
        local_steps(i)
        for g in range(GROUPS):
            order.append(("pass_out", i * GROUPS + g))
        if i == 0:
            for g in range(GROUPS):
                order.append(("global_norm", g))
                order.append(("global_transpose", g))
                order.append(("global_project", g))
            for t in range(TILES + 2):
                if t < TILES:
                    order.append(("global_scores", t))
                if 0 <= t - 1 < TILES:
                    order.append(("global_probs", t - 1))
                if 0 <= t - 2 < TILES:
                    order.append(("global_mix", t - 2))
    return order


def stage_banks(stage, m):
    if stage == "transpose_x":
        return ["xT"]
    if stage == "project":
        return ["q", "k", "v"]
    if stage == "transpose_qk":
        return ["qT", "kT"]
    if stage == "scores":
        return ["s0", "s1"]
    if stage == "transpose_probs":
        return ["p0", "p1"]
    if stage == "mix_values":
        return ["oT"]
    if stage == "attend_out":
        return ["y"]
    if stage == "ff_up":
        up = ["ffT"]
        for c in range(N_CHUNKS):
            up += [f"gate{c}", f"lin{c}"]
        return up
    if stage == "ff_down":
        return ["ff"]
    if stage == "global_transpose":
        return ["GxT"]
    if stage == "global_project":
        return ["Gq", "Gk", "Gv"]
    if stage == "global_scores":
        return [f"Gs{c}" for c in range(m // GROUP + 1)]
    if stage == "global_probs":
        return [f"Gp{c}" for c in range(m // GROUP + 1)]
    if stage == "global_mix":
        return ["Go"]
    return []


def build(nc, x_in, out, w):
    fp32, bf16 = mybir.dt.float32, mybir.dt.bfloat16
    ALU, ACT, AX = mybir.AluOpType, mybir.ActivationFunctionType, mybir.AxisListType
    ORDER = stage_order()

    fills = [(what, m) for stage, m in ORDER for what in stage_banks(stage, m)]
    fill = {f: k for k, f in enumerate(fills)}

    ctx = ExitStack()
    with ctx:
        def sb(name, shape, dt=fp32):
            return ctx.enter_context(nc.sbuf_tensor(name, shape, dt))

        first_sem = []

        def sem(name):
            s = ctx.enter_context(nc.semaphore(name))
            first_sem.append(s)
            return s

        wqkv = sb("wqkv", [P, LAYERS, 3 * INNER])
        wo = sb("wo", [P, LAYERS, PAIRS, D])
        w1 = sb("w1", [P, LAYERS, 2 * HID])
        w2 = sb("w2", [P, LAYERS, N_CHUNKS, D])
        b1 = sb("b1", [P, LAYERS, 2, N_CHUNKS])
        ln_g = sb("ln_g", [P, LAYERS])
        ln_b = sb("ln_b", [P, LAYERS])
        gw = sb("gw", [P, 3 * D])
        ident = sb("ident", [P, P])
        ident16 = sb("ident16", [P, P], bf16)
        mask_f = sb("mask_f", [P, 2 * 4 * P + P])
        mask16 = sb("mask16", [P, 2 * 4 * P + P], bf16)
        window_mask = mask16[:, 0:512]
        first_mask = mask16[:, 512:1024]
        causal_mask = mask16[:, 1024:1152]
        cos_raw = sb("cos_raw", [P, TILES, 2, HEAD_D])
        sin_raw = sb("sin_raw", [P, TILES, 2, HEAD_D])
        qk_gain = sb("qk_gain", [P, LAYERS, 2, 2, HEAD_D])
        cos_t = sb("cos_t", [P, LAYERS, TILES, 2, HEAD_D])
        sin_t = sb("sin_t", [P, LAYERS, TILES, 2, HEAD_D])
        minus_half = sb("minus_half", [P, 2 * HEADS])

        x = sb("x", [P, TILES, D])
        y = sb("y", [P, TILES, D])
        hT = sb("hT", [P, N_TOK + 1])
        v_odd = sb("v_odd", [P, TILES, INNER])
        v_even = sb("v_even", [P, TILES, INNER])
        kT = sb("kT", [P, PAIRS, WINDOW + N_TOK])
        qT = sb("qT", [P, 2, PAIRS, P])
        squares = sb("squares", [P, 2 * INNER])
        norm2 = sb("norm2", [P, 2, 2 * HEADS])
        inv_norm = sb("inv_norm", [P, 2, 2 * HEADS])
        rope_a = sb("rope_a", [P, 2, 2 * INNER])
        rope_b = sb("rope_b", [P, 2, 2 * INNER])
        roped = sb("roped", [P, 2, 2 * INNER])
        neg_max = sb("neg_max", [P, 2, HEADS])
        row_sum = sb("row_sum", [P, 2, HEADS])
        inv_sum = sb("inv_sum", [P, 2, HEADS])
        probs = sb("probs", [P, 2, HEADS, P])
        pT = sb("pT", [P, 2, HEADS, P])
        oT = sb("oT", [P, 2, PAIRS, P])
        shifted = sb("shifted", [P, TILES, D])
        stats = sb("stats", [P, GROUP, 6])
        mean_var = sb("mean_var", [P, GROUP, 2])
        var_eps = sb("var_eps", [P, GROUP])
        rstd = sb("rstd", [P, GROUP])
        normed = sb("normed", [P, GROUP, D])
        nT = sb("nT", [P, GROUP * P])
        gate = sb("gate", [P, N_CHUNKS, GROUP * P])
        hid = sb("hid", [P, N_CHUNKS, GROUP * P])
        g_xT = hid[:, 0, :]
        g_qT = sb("g_qT", [P, N_TOK])
        g_kT = sb("g_kT", [P, N_TOK])
        g_v = sb("g_v", [P, TILES, D])
        g_max = sb("g_max", [P, 2, 2])
        g_negmax = sb("g_negmax", [P, 2])
        g_sum = sb("g_sum", [P, 2, 2])
        g_total = sb("g_total", [P, 2])
        g_inv = sb("g_inv", [P, 2])
        g_probs = probs
        g_pT = pT
        y_new = sb("y_new", [P, 2])

        banks = [ctx.enter_context(nc.psum_tensor(f"bank{i}", [P, 512], fp32)) for i in range(BANKS)]

        loaded = sem("loaded")
        set_up = sem("set_up")
        zeroed = sem("zeroed")
        seq_done = sem("seq_done")
        seq_idle = sem("seq_idle")
        seq_go = sem("seq_go")
        cleared_from = len(first_sem)

        full = [sem(f"full{b}") for b in range(BANKS)]
        x_loaded = sem("x_loaded")
        hT_ready = sem("hT_ready")
        squares_ready = sem("squares_ready")
        norm2_ready = sem("norm2_ready")
        norm2_clipped = sem("norm2_clipped")
        inv_norm_ready = sem("inv_norm_ready")
        products_ready = sem("products_ready")
        rope_sum_ready = sem("rope_sum_ready")
        roped_ready = sem("roped_ready")
        qT_ready = sem("qT_ready")
        kT_ready = sem("kT_ready")
        v_ready = sem("v_ready")
        v_shifted = [sem(f"v_shifted{i}") for i in range(4)]
        max_ready = sem("max_ready")
        exp_ready = sem("exp_ready")
        inv_sum_ready = sem("inv_sum_ready")
        probs_ready = sem("probs_ready")
        pT0_ready = sem("pT0_ready")
        pT1_ready = sem("pT1_ready")
        oT_ready = sem("oT_ready")
        attended = sem("attended")
        low_copied = sem("low_copied")
        y_shifted = sem("y_shifted")
        stats_ready = sem("stats_ready")
        mean_var_ready = sem("mean_var_ready")
        eps_added = sem("eps_added")
        rstd_ready = sem("rstd_ready")
        normed_ready = sem("normed_ready")
        nT_ready = sem("nT_ready")
        gate_ready = sem("gate_ready")
        hid_ready = sem("hid_ready")
        ff_added = sem("ff_added")
        x_updated = sem("x_updated")
        gxT_ready = sem("gxT_ready")
        gqkv_ready = sem("gqkv_ready")
        gmax_part = sem("gmax_part")
        gmax_ready = sem("gmax_ready")
        gexp_ready = sem("gexp_ready")
        gtotal_ready = sem("gtotal_ready")
        ginv_ready = sem("ginv_ready")
        gpT_ready = sem("gpT_ready")
        g_added = sem("g_added")
        stored = sem("stored")
        cleared = [s.num for s in first_sem[cleared_from:]]
        assert cleared == list(range(cleared[0], cleared[0] + len(cleared)))

        def pass_of(n):
            return n // (LAYERS * TILES)

        def layer_of(n):
            return n // TILES % LAYERS

        ln_unit = {}
        for stage, m in ORDER:
            if stage in ("input_norm", "ff_norm", "global_norm"):
                ln_unit[stage, m] = len(ln_unit)
        through = [(stage, m) for stage, m in ORDER if stage in ("ff_norm", "global_norm")]
        before = dict(zip(through[1:], through))
        g_units = {}
        for t in range(TILES):
            for c in range(t // GROUP + 1):
                g_units[t, c] = len(g_units) + 1

        def read_by(what, m):
            c = int(what[-1]) if what[-1].isdigit() else 0
            return {
                "xT": [(hT_ready, 2 * m + 2)],
                "q": [(products_ready, 6 * m + 3)],
                "k": [(products_ready, 6 * m + 6)],
                "v": [(v_ready, m + 1)],
                "qT": [(qT_ready, m + 1)],
                "kT": [(kT_ready, m + 1)],
                "s": [(exp_ready, 2 * m + c + 1)],
                "p": [((pT0_ready, pT1_ready)[c % 2], m + 1)],
                "oT": [(oT_ready, m + 1)],
                "y": [(attended, m + 1)],
                "ffT": [(nT_ready, m + 1)],
                "gate": [(gate_ready, N_CHUNKS * m + c + 1)],
                "lin": [(hid_ready, N_CHUNKS * m + c + 1)],
                "ff": [(ff_added, m + 1)],
                "GxT": [(gxT_ready, m + 1)],
                "Gq": [(gqkv_ready, 3 * m + 1)],
                "Gk": [(gqkv_ready, 3 * m + 2)],
                "Gv": [(gqkv_ready, 3 * m + 3)],
                "Gs": [(gexp_ready, g_units.get((m, c)))],
                "Gp": [(gpT_ready, g_units.get((m, c)))],
                "Go": [(g_added, m + 1)],
            }[what.rstrip("0123456789")]

        def bank(what, m):
            return banks[fill[what, m] % BANKS]

        def take_bank(pe, what, m):
            k = fill[what, m]
            if k >= BANKS:
                for semaphore, count in read_by(*fills[k - BANKS]):
                    pe.wait_ge(semaphore, count)
            return banks[k % BANKS]

        def filled(ins, what, m):
            ins.then_inc(full[fill[what, m] % BANKS], 1)

        def wait_full(eng, what, m):
            k = fill[what, m]
            eng.wait_ge(full[k % BANKS], k // BANKS + 1)
            return banks[k % BANKS]

        def end_sequence(eng, it):
            eng.sem_inc(seq_done, 1)
            eng.wait_ge(seq_go, it + 1)

        block = ctx.enter_context(nc.Block())

        @block.sync
        def _(sp):
            for dst, src in ((ident[:, :], w["ident"]), (wqkv[:, :, :], w["wqkv"]),
                             (cos_raw[:, :, :, :], w["cos"]), (sin_raw[:, :, :, :], w["sin"]),
                             (qk_gain[:, :, :, :, :], w["qk_gain"]), (mask_f[:, :], w["masks"]),
                             (wo[:, :, :, :], w["wo"]), (w1[:, :, :], w["w1"]),
                             (w2[:, :, :, :], w["w2"]), (b1[:, :, :, :], w["b1"]),
                             (ln_g[:, :], w["ln_g"]), (ln_b[:, :], w["ln_b"]), (gw[:, :], w["gw"])):
                sp.dma_start(dst, src).then_inc(loaded, 16)

            with sp.Fori(0, SEQS) as it:
                sp.dma_start(x[:, :, :], x_in[bass.ds(it, 1), :, :].rearrange("s (t p) d -> p (s t) d", p=P)).then_inc(x_loaded, 16)
                for stage, m in ORDER:
                    if stage == "project":
                        t = m % TILES
                        sp.wait_ge(v_ready, m + 1)
                        if m >= TILES:
                            wait_full(sp, "oT", m - TILES)
                        if t > 0:
                            sp.dma_start(v_even[0:64, t, :], v_odd[64:128, t - 1, :]).then_inc(v_shifted[m % 4], 16)
                        sp.dma_start(v_even[64:128, t, :], v_odd[0:64, t, :]).then_inc(v_shifted[m % 4], 16)
                    if stage == "ff_norm":
                        g = m % GROUPS
                        a = GROUP * g
                        sp.wait_ge(attended, GROUP * (m + 1))
                        up = shifted[:, :, 64:128]
                        src = y[:, :, 64:128]
                        sp.dma_start(up[16:128, a:a + GROUP, :], src[15:127, a:a + GROUP, :]).then_inc(y_shifted, 16)
                        sp.dma_start(up[1:16, a:a + GROUP, :], src[0:15, a:a + GROUP, :]).then_inc(y_shifted, 16)
                        last = min(GROUP, TILES - 1 - a)
                        sp.dma_start(up[0:1, a + 1:a + 1 + last, :], src[127:128, a:a + last, :]).then_inc(y_shifted, 16)
                    if stage == "pass_out" and m >= GROUPS:
                        g = m % GROUPS
                        sp.wait_ge(x_updated, m + 1)
                        sp.dma_start(out[bass.ds(it, 1), g * 512:(g + 1) * 512, :].rearrange("s (t p) d -> p (s t) d", p=P),
                                     x[:, g * GROUP:(g + 1) * GROUP, :]).then_inc(stored, 16)
                sp.wait_ge(stored, 16 * GROUPS)
                sp.wait_ge(seq_done, 4 * it + 4)
                sp.sem_inc(seq_idle, 1)
                sp.sem_clear(range(cleared[0], cleared[-1] + 1))
                sp.sem_inc(seq_go, 1)

        @block.tensor
        def _(pe):
            pe.wait_ge(loaded, 16 * 13)
            pe.wait_ge(zeroed, ZEROED)
            pe.wait_ge(set_up, 2)
            with pe.Fori(0, SEQS) as it:
                for stage, m in ORDER:
                    t = m % TILES
                    lay = layer_of(m)
                    if stage == "transpose_x":
                        if lay == 0:
                            pe.wait_ge(normed_ready, ln_unit["input_norm", pass_of(m) * GROUPS + t // GROUP] + 1)
                        else:
                            pe.wait_ge(ff_added, m // GROUP - GROUPS + 1)
                        b = take_bank(pe, "xT", m)
                        filled(pe.transpose(b[:, 0:P], y[:, t, :], ident[:, :]), "xT", m)
                    if stage == "project":
                        pe.wait_ge(hT_ready, 2 * m + 2)
                        for j, what in enumerate("qkv"):
                            b = take_bank(pe, what, m)
                            mm = pe.matmul(b[:, :], hT[:, t * P:(t + 1) * P], wqkv[:, lay, j * INNER:(j + 1) * INNER],
                                           start=True, stop=True)
                            filled(mm, what, m)
                    if stage == "transpose_qk":
                        pe.wait_ge(roped_ready, m + 1)
                        for j, what in enumerate(("qT", "kT")):
                            b = take_bank(pe, what, m)
                            for c in range(PAIRS):
                                mm = pe.transpose(b[:, c * P:(c + 1) * P],
                                                  roped[:, m % 2, j * INNER + c * P:j * INNER + (c + 1) * P], ident[:, :])
                            filled(mm, what, m)
                    if stage == "scores":
                        pe.wait_ge(qT_ready, m + 1)
                        pe.wait_ge(kT_ready, m + 1)
                        for win in range(2):
                            b = take_bank(pe, f"s{win}", m)
                            mask = first_mask if t == 0 and win == 0 else window_mask
                            pe.matmul(b[:, :], ident16[:, :], mask, start=True, stop=True, skip_group_check=True)
                            k0 = t * P + win * WINDOW
                            for c in range(PAIRS):
                                for h in range(2):
                                    r = slice(64 * h, 64 * h + 64)
                                    mm = pe.matmul(b[r, c * P:(c + 1) * P], qT[r, m % 2, c, win * 64:win * 64 + 64],
                                                   kT[r, c, k0:k0 + 2 * WINDOW], start=False, stop=True,
                                                   skip_group_check=True)
                            filled(mm, f"s{win}", m)
                    if stage == "transpose_probs":
                        for win in range(2):
                            pe.wait_ge(probs_ready, 2 * m + win + 1)
                            b = take_bank(pe, f"p{win}", m)
                            for c in range(PAIRS):
                                mm = pe.transpose(b[:, c * P:(c + 1) * P], probs[:, m % 2, win * PAIRS + c, :], ident[:, :])
                            filled(mm, f"p{win}", m)
                    if stage == "mix_values":
                        b = take_bank(pe, "oT", m)
                        for win in range(2):
                            pe.wait_ge((pT0_ready, pT1_ready)[win], m + 1)
                            if win == 0:
                                same = [i for i in range(m + 1) if i % 4 == m % 4]
                                pe.wait_ge(v_shifted[m % 4], sum(32 if i % TILES else 16 for i in same))
                            v = (v_even, v_odd)[win]
                            for c in range(PAIRS):
                                for h in range(2):
                                    head = 2 * c + h
                                    mm = pe.matmul(b[64 * h:64 * h + 64, c * P + win * 64:c * P + win * 64 + 64],
                                                   v[:, t, head * 64:head * 64 + 64],
                                                   pT[:, m % 2, win * PAIRS + c, 64 * h:64 * h + 64],
                                                   start=True, stop=True, skip_group_check=True)
                        filled(mm, "oT", m)
                    if stage == "attend_out":
                        pe.wait_ge(oT_ready, m + 1)
                        b = take_bank(pe, "y", m)
                        for c in range(PAIRS):
                            mm = pe.matmul(b[:, 0:D], oT[:, m % 2, c, :], wo[:, lay, c, :],
                                           start=(c == 0), stop=(c == PAIRS - 1))
                        filled(mm, "y", m)
                    if stage in ("ff_up", "ff_down"):
                        lay = m // GROUPS % LAYERS
                    if stage == "ff_up":
                        pe.wait_ge(normed_ready, ln_unit["ff_norm", m] + 1)
                        b = take_bank(pe, "ffT", m)
                        for i in range(GROUP):
                            mm = pe.transpose(b[:, i * P:(i + 1) * P], normed[:, i, :], ident[:, :])
                        filled(mm, "ffT", m)
                        pe.wait_ge(nT_ready, m + 1)
                        for c, (at, size) in enumerate(HID_CHUNKS):
                            for what, base in ((f"gate{c}", HID), (f"lin{c}", 0)):
                                b = take_bank(pe, what, m)
                                mm = pe.matmul(b[0:size, :], w1[:, lay, base + at:base + at + size], nT[:, :],
                                               start=True, stop=True)
                                filled(mm, what, m)
                    if stage == "ff_down":
                        pe.wait_ge(hid_ready, N_CHUNKS * (m + 1))
                        b = take_bank(pe, "ff", m)
                        for i in range(GROUP):
                            for c, (at, size) in enumerate(HID_CHUNKS):
                                rows = size + 1 if c == N_CHUNKS - 1 else size
                                mm = pe.matmul(b[:, i * P:(i + 1) * P], hid[0:rows, c, i * P:(i + 1) * P],
                                               w2[0:rows, lay, c, :], start=(c == 0), stop=(c == N_CHUNKS - 1))
                        filled(mm, "ff", m)
                    if stage == "global_transpose":
                        pe.wait_ge(normed_ready, ln_unit["global_norm", m] + 1)
                        b = take_bank(pe, "GxT", m)
                        for i in range(GROUP):
                            mm = pe.transpose(b[:, i * P:(i + 1) * P], normed[:, i, :], ident[:, :])
                        filled(mm, "GxT", m)
                    if stage == "global_project":
                        pe.wait_ge(gxT_ready, m + 1)
                        for j, what in enumerate(("Gq", "Gk")):
                            b = take_bank(pe, what, m)
                            filled(pe.matmul(b[:, :], gw[:, j * D:(j + 1) * D], nT[:, :], start=True, stop=True), what, m)
                        b = take_bank(pe, "Gv", m)
                        for i in range(GROUP):
                            mm = pe.matmul(b[:, i * P:(i + 1) * P], nT[:, i * P:(i + 1) * P], gw[:, 2 * D:3 * D],
                                           start=True, stop=True)
                        filled(mm, "Gv", m)
                    if stage == "global_scores":
                        pe.wait_ge(gqkv_ready, 3 * (m // GROUP + 1))
                        for c in range(m // GROUP + 1):
                            b = take_bank(pe, f"Gs{c}", m)
                            keys = min((c + 1) * 512, (m + 1) * P) - c * 512
                            diagonal = c == m // GROUP
                            mm = pe.matmul(b[:, 0:keys], g_qT[:, m * P:(m + 1) * P], g_kT[:, c * 512:c * 512 + keys],
                                           start=True, stop=True)
                            if diagonal:
                                mm = pe.matmul(b[:, keys - P:keys], ident16[:, :], causal_mask, start=False, stop=True,
                                               skip_group_check=True)
                            filled(mm, f"Gs{c}", m)
                    if stage == "global_probs":
                        for c in range(m // GROUP + 1):
                            pe.wait_ge(gexp_ready, g_units[m, c])
                            b = take_bank(pe, f"Gp{c}", m)
                            for j in range(min(GROUP, m + 1 - c * GROUP)):
                                mm = pe.transpose(b[:, j * P:(j + 1) * P], g_probs[:, m % 2, c * GROUP + j, :], ident[:, :])
                            filled(mm, f"Gp{c}", m)
                    if stage == "global_mix":
                        b = take_bank(pe, "Go", m)
                        for j in range(m + 1):
                            if j % GROUP == 0:
                                pe.wait_ge(gpT_ready, g_units[m, j // GROUP])
                            mm = pe.matmul(b[:, 0:D], g_pT[:, m % 2, j, :], g_v[:, j, :], start=(j == 0), stop=(j == m))
                        filled(mm, "Go", m)
                end_sequence(pe, it)

        @block.scalar
        def _(act):
            act.wait_ge(loaded, 16 * 13)
            act.wait_ge(zeroed, ZEROED)

            def wait_nT_used(stage, m):
                if (stage, m) in before:
                    kind, i = before[stage, m]
                    wait_full(act, f"lin{N_CHUNKS - 1}" if kind == "ff_norm" else "Gv", i)

            with act.Fori(0, SEQS) as it:
                for stage, m in ORDER:
                    t = m % TILES
                    lay = layer_of(m)
                    if stage == "transpose_x":
                        b = wait_full(act, "xT", m)
                        act.activation(hT[0:64, t * P:(t + 1) * P], b[0:64, 0:P], ACT.Copy).then_inc(hT_ready, 1)
                        ins = act.activation(hT[64:128, t * P + 1:(t + 1) * P + 1], b[64:128, 0:P], ACT.Copy)
                        ins.then_inc(hT_ready, 1)
                    if stage == "project":
                        if m:
                            act.wait_ge(norm2_ready, m)
                        for j, what in enumerate("qk"):
                            b = wait_full(act, what, m)
                            ins = act.activation(squares[:, j * INNER:(j + 1) * INNER], b[:, :], ACT.Square)
                            ins.then_inc(squares_ready, 1)
                        b = wait_full(act, "v", m)
                        if m >= TILES:
                            same = [i for i in range(m - TILES + 2) if i % 4 == (m + 1) % 4]
                            act.wait_ge(v_shifted[(m + 1) % 4], sum(32 if i % TILES else 16 for i in same))
                        ins = act.activation(v_odd[:, t, :], b[:, :], ACT.Copy)
                        ins.then_inc(v_ready, 1)
                    if stage == "transpose_qk":
                        b = wait_full(act, "qT", m)
                        ins = act.activation(qT[:, m % 2, :, :], b[:, :].rearrange("p (c q) -> p c q", c=PAIRS), ACT.Copy)
                        ins.then_inc(qT_ready, 1)
                        b = wait_full(act, "kT", m)
                        ins = act.activation(kT[:, :, WINDOW + t * P:WINDOW + (t + 1) * P],
                                             b[:, :].rearrange("p (c q) -> p c q", c=PAIRS), ACT.Copy)
                        ins.then_inc(kT_ready, 1)
                    if stage == "scores":
                        for win in range(2):
                            act.wait_ge(max_ready, 2 * m + win + 1)
                            b = bank(f"s{win}", m)
                            for c in range(PAIRS):
                                i = win * PAIRS + c
                                ins = act.activation(probs[:, m % 2, i, :], b[:, c * P:(c + 1) * P], ACT.Exp,
                                                     bias=neg_max[:, m % 2, i:i + 1], scale=1.0,
                                                     accum_out=row_sum[:, m % 2, i:i + 1])
                            ins.then_inc(exp_ready, 1)
                    if stage == "transpose_probs":
                        b = wait_full(act, "p0", m)
                        ins = act.activation(pT[:, m % 2, 0:PAIRS, :], b[:, :].rearrange("p (c q) -> p c q", c=PAIRS), ACT.Copy)
                        ins.then_inc(pT0_ready, 1)
                    if stage == "ff_up":
                        lay = m // GROUPS % LAYERS
                        b = wait_full(act, "ffT", m)
                        wait_nT_used("ff_norm", m)
                        ins = act.activation(nT[:, :], b[:, :], ACT.Identity, bias=ln_b[:, lay:lay + 1], scale=ln_g[:, lay:lay + 1])
                        ins.then_inc(nT_ready, 1)
                        for c, (at, size) in enumerate(HID_CHUNKS):
                            b = wait_full(act, f"gate{c}", m)
                            if m:
                                act.wait_ge(hid_ready, N_CHUNKS * (m - 1) + c + 1)
                            ins = act.activation(gate[0:size, c, :], b[0:size, :], ACT.Gelu, bias=b1[0:size, lay, 1, c:c + 1])
                            ins.then_inc(gate_ready, 1)
                    if stage == "global_transpose":
                        b = wait_full(act, "GxT", m)
                        wait_nT_used("global_norm", m)
                        ins = act.activation(nT[:, :], b[:, :], ACT.Copy)
                        ins.then_inc(gxT_ready, 1)
                    if stage == "global_project":
                        a = m * GROUP
                        for what, dst in (("Gq", g_qT[:, a * P:a * P + 512]), ("Gk", g_kT[:, a * P:a * P + 512]),
                                          ("Gv", g_v[:, a:a + GROUP, :].rearrange("p t d -> p (t d)"))):
                            b = wait_full(act, what, m)
                            ins = act.activation(dst, b[:, :], ACT.Copy)
                            ins.then_inc(gqkv_ready, 1)
                    if stage == "global_scores":
                        act.wait_ge(gmax_ready, m + 1)
                        for c in range(m // GROUP + 1):
                            b = bank(f"Gs{c}", m)
                            keys = min((c + 1) * 512, (m + 1) * P) - c * 512
                            ins = act.activation(g_probs[:, m % 2, c * GROUP:c * GROUP + keys // P, :].rearrange("p a b -> p (a b)"),
                                                 b[:, 0:keys], ACT.Exp, bias=g_negmax[:, m % 2:m % 2 + 1], scale=SCORE_SCALE,
                                                 accum_out=g_sum[:, m % 2, c:c + 1])
                            ins.then_inc(gexp_ready, 1)
                end_sequence(act, it)

        @block.vector
        def _(dve):
            dve.wait_ge(loaded, 16 * 13)
            dve.tensor_copy(ident16[:, :], ident[:, :]).then_inc(set_up, 1)
            dve.tensor_copy(mask16[:, :], mask_f[:, :]).then_inc(set_up, 1)
            for lay in range(LAYERS):
                for raw, table, j in ((cos_raw, cos_t, 0), (sin_raw, sin_t, 1)):
                    for i in range(2):
                        gain = qk_gain[:, lay, j, i, :].unsqueeze(1).to_broadcast([P, TILES, HEAD_D])
                        dve.tensor_tensor(table[:, lay, :, i, :], raw[:, :, i, :], gain, ALU.mult).then_inc(set_up, 1)
            dve.wait_ge(set_up, 2 + 4 * LAYERS)
            dve.wait_ge(zeroed, ZEROED)

            def norm_group(stage, m, src, dst):
                u = ln_unit[stage, m]
                for i in range(GROUP):
                    dve.bn_stats(stats[:, i, :], src[:, i, :]).then_inc(stats_ready, 1)
                dve.wait_ge(stats_ready, GROUP * (u + 1))
                for i in range(GROUP):
                    dve.bn_aggr(mean_var[:, i, :], stats[:, i, :]).then_inc(mean_var_ready, 1)
                dve.wait_ge(rstd_ready, u + 1)
                if (stage, m) in before:
                    kind, i = before[stage, m]
                    wait_full(dve, "ffT" if kind == "ff_norm" else "GxT", i)
                for i in range(GROUP):
                    ins = dve.tensor_scalar(dst[:, i, :], src[:, i, :], mean_var[:, i, 0:1], rstd[:, i:i + 1],
                                            ALU.subtract, ALU.mult)
                ins.then_inc(normed_ready, 1)

            with dve.Fori(0, SEQS) as it:
                for stage, m in ORDER:
                    t = m % TILES
                    lay = layer_of(m)
                    if stage == "input_norm":
                        a = m % GROUPS * GROUP
                        if m == 0:
                            dve.wait_ge(x_loaded, 16)
                        if m >= GROUPS:
                            dve.wait_ge(g_added, a + GROUP)
                        norm_group(stage, m, x[:, a:a + GROUP, :], y[:, a:a + GROUP, :])
                    if stage == "project":
                        if m >= 2:
                            dve.wait_ge(rope_sum_ready, m - 1)
                        for j, what in enumerate("qk"):
                            dve.wait_ge(squares_ready, 2 * m + j + 1)
                            b = bank(what, m)
                            a_out = rope_a[:, m % 2, j * INNER:(j + 1) * INNER]
                            b_out = rope_b[:, m % 2, j * INNER:(j + 1) * INNER]
                            cos = cos_t[:, lay, t, j, :].unsqueeze(1).to_broadcast([P, HEADS, HEAD_D])
                            dve.tensor_tensor(a_out.rearrange("p (h d) -> p h d", h=HEADS),
                                              b[:, :].rearrange("p (h d) -> p h d", h=HEADS), cos, ALU.mult).then_inc(products_ready, 1)
                            for half in range(2):
                                o, i = half * HALF, (1 - half) * HALF
                                sin = sin_t[:, lay, t, j, o:o + HALF].unsqueeze(1).to_broadcast([P, HEADS, HALF])
                                ins = dve.tensor_tensor(b_out.rearrange("p (h d) -> p h d", h=HEADS)[:, :, o:o + HALF],
                                                        b[:, :].rearrange("p (h d) -> p h d", h=HEADS)[:, :, i:i + HALF],
                                                        sin, ALU.mult)
                                ins.then_inc(products_ready, 1)
                        if m >= 2:
                            dve.wait_ge(norm2_clipped, m - 1)
                        dve.tensor_reduce(norm2[:, m % 2, :], squares[:, :].rearrange("p (h d) -> p h d", d=HEAD_D),
                                          AX.X, ALU.add).then_inc(norm2_ready, 1)
                    if stage == "rope_finish":
                        dve.wait_ge(rope_sum_ready, m + 1)
                        dve.wait_ge(inv_norm_ready, m + 1)
                        if m >= 2:
                            wait_full(dve, "kT", m - 2)
                        inv = inv_norm[:, m % 2, :].unsqueeze(2).to_broadcast([P, 2 * HEADS, HEAD_D])
                        dve.tensor_tensor(roped[:, m % 2, :].rearrange("p (h d) -> p h d", d=HEAD_D),
                                          rope_a[:, m % 2, :].rearrange("p (h d) -> p h d", d=HEAD_D), inv,
                                          ALU.mult).then_inc(roped_ready, 1)
                    if stage == "scores":
                        for win in range(2):
                            b = wait_full(dve, f"s{win}", m)
                            dve.tensor_reduce(neg_max[:, m % 2, win * PAIRS:(win + 1) * PAIRS],
                                              b[:, :].rearrange("p (c k) -> p c k", c=PAIRS), AX.X, ALU.max,
                                              negate=True).then_inc(max_ready, 1)
                    if stage == "probs_finish":
                        for win in range(2):
                            dve.wait_ge(exp_ready, 2 * m + win + 1)
                            dve.reciprocal(inv_sum[:, m % 2, win * PAIRS:(win + 1) * PAIRS],
                                           row_sum[:, m % 2, win * PAIRS:(win + 1) * PAIRS]).then_inc(inv_sum_ready, 1)
                    if stage == "transpose_probs":
                        b = wait_full(dve, "p1", m)
                        ins = dve.tensor_copy(pT[:, m % 2, PAIRS:, :], b[:, :].rearrange("p (c q) -> p c q", c=PAIRS))
                        ins.then_inc(pT1_ready, 1)
                    if stage == "mix_values":
                        b = wait_full(dve, "oT", m)
                        ins = dve.tensor_copy(oT[:, m % 2, :, :], b[:, :].rearrange("p (c q) -> p c q", c=PAIRS))
                        ins.then_inc(oT_ready, 1)
                    if stage == "attend_out":
                        b = wait_full(dve, "y", m)
                        ins = dve.tensor_tensor(y[:, t, :], b[:, 0:D], y[:, t, :], ALU.add)
                        ins.then_inc(attended, 1)
                    if stage == "ff_norm":
                        a = m % GROUPS * GROUP
                        dve.wait_ge(low_copied, m + 1)
                        dve.wait_ge(y_shifted, 48 * (m + 1))
                        norm_group(stage, m, shifted[:, a:a + GROUP, :], normed[:, :, :])
                    if stage == "ff_up":
                        lay = m // GROUPS % LAYERS
                        for c, (at, size) in enumerate(HID_CHUNKS):
                            b = wait_full(dve, f"lin{c}", m)
                            dve.wait_ge(gate_ready, N_CHUNKS * m + c + 1)
                            ins = dve.scalar_tensor_tensor(hid[0:size, c, :], b[0:size, :], b1[0:size, lay, 0, c:c + 1],
                                                           gate[0:size, c, :], ALU.add, ALU.mult)
                            ins.then_inc(hid_ready, 1)
                    if stage == "ff_down":
                        a = m % GROUPS * GROUP
                        b = wait_full(dve, "ff", m)
                        rows = y[:, a:a + GROUP, :].rearrange("p t d -> p (t d)")
                        ins = dve.tensor_tensor(rows, b[:, :], rows, ALU.add)
                        ins.then_inc(ff_added, 1)
                    if stage == "pass_out":
                        g = m % GROUPS
                        i = m // GROUPS
                        dve.wait_ge(ff_added, (i * LAYERS + LAYERS - 1) * GROUPS + g + 1)
                        rows = slice(g * GROUP, (g + 1) * GROUP)
                        dve.scalar_tensor_tensor(x[:, rows, :].rearrange("p t d -> p (t d)"),
                                                 y[:, rows, :].rearrange("p t d -> p (t d)"), 0.5,
                                                 x[:, rows, :].rearrange("p t d -> p (t d)"),
                                                 ALU.mult, ALU.add).then_inc(x_updated, 1)
                    if stage == "global_norm":
                        a = m * GROUP
                        dve.wait_ge(x_updated, m + 1)
                        norm_group(stage, m, x[:, a:a + GROUP, :], normed[:, :, :])
                    if stage == "global_scores":
                        for c in range(m // GROUP + 1):
                            b = wait_full(dve, f"Gs{c}", m)
                            keys = min((c + 1) * 512, (m + 1) * P) - c * 512
                            dve.tensor_reduce(g_max[:, m % 2, c:c + 1], b[:, 0:keys], AX.X, ALU.max).then_inc(gmax_part, 1)
                        dve.wait_ge(gmax_part, g_units[m, m // GROUP])
                        if m < GROUP:
                            ins = dve.tensor_scalar(g_negmax[:, m % 2:m % 2 + 1], g_max[:, m % 2, 0:1], -SCORE_SCALE, None, ALU.mult)
                        else:
                            ins = dve.tensor_scalar(g_negmax[:, m % 2:m % 2 + 1], g_max[:, m % 2, 0:1],
                                                    g_max[:, m % 2, 1:2], -SCORE_SCALE, ALU.max, ALU.mult)
                        ins.then_inc(gmax_ready, 1)
                    if stage == "global_probs":
                        for c in range(m // GROUP + 1):
                            b = wait_full(dve, f"Gp{c}", m)
                            tiles = min(GROUP, m + 1 - c * GROUP)
                            ins = dve.tensor_copy(g_pT[:, m % 2, c * GROUP:c * GROUP + tiles, :].rearrange("p a b -> p (a b)"),
                                                  b[:, 0:tiles * P])
                            ins.then_inc(gpT_ready, 1)
                        dve.wait_ge(gexp_ready, g_units[m, m // GROUP])
                        total = g_sum[:, m % 2, 0:1]
                        if m >= GROUP:
                            total = g_total[:, m % 2:m % 2 + 1]
                            dve.tensor_tensor(total, g_sum[:, m % 2, 0:1], g_sum[:, m % 2, 1:2], ALU.add).then_inc(gtotal_ready, 1)
                            dve.wait_ge(gtotal_ready, m - GROUP + 1)
                        dve.reciprocal(g_inv[:, m % 2:m % 2 + 1], total).then_inc(ginv_ready, 1)
                    if stage == "global_mix":
                        b = wait_full(dve, "Go", m)
                        dve.wait_ge(ginv_ready, m + 1)
                        ins = dve.scalar_tensor_tensor(x[:, m, :], b[:, 0:D], g_inv[:, m % 2:m % 2 + 1], x[:, m, :],
                                                       ALU.mult, ALU.add)
                        ins.then_inc(g_added, 1)
                end_sequence(dve, it)

        @block.gpsimd
        def _(pool):
            for i, (part, value) in enumerate((
                    (hT[64:128, 0:1], 0.0),
                    (kT[:, :, 0:WINDOW], 0.0),
                    (v_even[0:64, 0, :], 0.0),
                    (shifted[0:1, 0, 64:128], 0.0),
                    (hid[64:128, N_CHUNKS - 1, :], 1.0),
                    (minus_half[:, :], -0.5))):
                if i:
                    pool.wait_ge(zeroed, i)
                pool.memset(part, value).then_inc(zeroed, 1)
            pool.wait_ge(zeroed, ZEROED)
            with pool.Fori(0, SEQS) as it:
                for stage, m in ORDER:
                    if stage == "project":
                        pool.wait_ge(norm2_ready, m + 1)
                        if m >= 2:
                            pool.wait_ge(roped_ready, m - 1)
                        pool.tensor_scalar(inv_norm[:, m % 2, :], norm2[:, m % 2, :], NORM2_MIN, None, ALU.max).then_inc(norm2_clipped, 1)
                        pool.wait_ge(norm2_clipped, m + 1)
                        pool.tensor_tensor(inv_norm[:, m % 2, :], inv_norm[:, m % 2, :], minus_half[:, :], ALU.pow).then_inc(inv_norm_ready, 1)
                        pool.wait_ge(products_ready, 6 * (m + 1))
                        pool.tensor_tensor(rope_a[:, m % 2, :], rope_a[:, m % 2, :], rope_b[:, m % 2, :], ALU.add).then_inc(rope_sum_ready, 1)
                    if stage == "probs_finish":
                        for win in range(2):
                            pool.wait_ge(inv_sum_ready, 2 * m + win + 1)
                            p = probs[:, m % 2, win * PAIRS:(win + 1) * PAIRS, :]
                            inv = inv_sum[:, m % 2, win * PAIRS:(win + 1) * PAIRS].unsqueeze(2).to_broadcast([P, PAIRS, P])
                            pool.tensor_tensor(p, p, inv, ALU.mult).then_inc(probs_ready, 1)
                    if stage == "ff_norm":
                        a = m % GROUPS * GROUP
                        pool.wait_ge(attended, GROUP * (m + 1))
                        pool.tensor_copy(shifted[:, a:a + GROUP, 0:64], y[:, a:a + GROUP, 0:64]).then_inc(low_copied, 1)
                    if (stage, m) in ln_unit:
                        u = ln_unit[stage, m]
                        pool.wait_ge(mean_var_ready, GROUP * (u + 1))
                        pool.tensor_scalar(var_eps[:, :], mean_var[:, :, 1], LN_EPS, None, ALU.add).then_inc(eps_added, 1)
                        pool.wait_ge(eps_added, u + 1)
                        if u:
                            pool.wait_ge(normed_ready, u)
                        pool.tensor_tensor(rstd[:, :], var_eps[:, :], minus_half[:, 0:GROUP], ALU.pow).then_inc(rstd_ready, 1)
                end_sequence(pool, it)


def kernel(L0_attn_x, L0_attn_W_qkv, L0_ffn_wqkv, L0_ffn_q_scale, L0_ffn_k_scale, L0_ffn_wo, L0_ffn_ln_g,
           L0_ffn_ln_b, L0_ffn_w1, L0_ffn_b1, L0_ffn_w2, L0_ffn_b2):
    import concourse.bacc as bacc
    from concourse.bass_utils import run_bass_kernel_spmd

    f = np.float32
    half_idx = np.arange(0, HEAD_D, 2, dtype=f)
    inv_freq = (f(1.0) / f(10000.0) ** (half_idx / f(HEAD_D))).astype(f)
    pos = np.arange(N_TOK, dtype=f)
    angle = pos[:, None] * inv_freq[None, :]
    base = ((half_idx + f(0.4 * HEAD_D)) / f(1.4 * HEAD_D)).astype(f)
    xpos = base[None, :] ** ((pos - N_TOK // 2) / f(WINDOW // 2))[:, None]
    angle, xpos = (np.concatenate([a, a], axis=1) for a in (angle, xpos))
    sign = np.where(np.arange(HEAD_D) < HALF, f(-1), f(1))
    qk_scale = f(8.0)
    cos = np.stack([qk_scale * np.cos(angle) * xpos, np.cos(angle) / xpos], axis=1)
    sin = np.stack([qk_scale * np.sin(angle) * xpos * sign, np.sin(angle) / xpos * sign], axis=1)
    cos, sin = (np.ascontiguousarray(a.reshape(TILES, P, 2, HEAD_D).transpose(1, 0, 2, 3).astype(f)) for a in (cos, sin))
    i, j = np.arange(P)[:, None] % WINDOW, np.arange(P)[None, :]
    inside = (j >= i) & (j <= i + WINDOW)
    window = np.where(inside, f(0), f(MASKED))
    first = np.where(inside & (j >= WINDOW), f(0), f(MASKED))
    causal = np.where(j <= np.arange(P)[:, None], f(0), f(MASKED))
    masks = np.concatenate([np.tile(window, (1, 4)), np.tile(first, (1, 4)), causal], axis=1).astype(f)

    def swap(a):
        return np.concatenate([a[:, HALF:], a[:, :HALF]], axis=1)

    qs, ks = np.asarray(L0_ffn_q_scale), np.asarray(L0_ffn_k_scale)
    gain = np.stack([np.stack([qs, ks], axis=1), np.stack([swap(qs), swap(ks)], axis=1)], axis=1)
    b1 = np.asarray(L0_ffn_b1)
    b1_cols = np.zeros((P, LAYERS, 2, N_CHUNKS), f)
    w2 = np.asarray(L0_ffn_w2)
    w2_rows = np.zeros((P, LAYERS, N_CHUNKS, D), f)
    for c, (at, size) in enumerate(HID_CHUNKS):
        for part in range(2):
            b1_cols[:size, :, part, c] = b1[:, part * HID + at:part * HID + at + size].T
        w2_rows[:size, :, c, :] = w2[:, at:at + size, :].transpose(1, 0, 2)
    w2_rows[B2_ROW, :, N_CHUNKS - 1, :] = np.asarray(L0_ffn_b2)
    arrays = {
        "x": np.asarray(L0_attn_x),
        "wqkv": np.asarray(L0_ffn_wqkv).transpose(1, 0, 2),
        "wo": np.asarray(L0_ffn_wo).reshape(LAYERS, PAIRS, P, D).transpose(2, 0, 1, 3),
        "w1": np.asarray(L0_ffn_w1).transpose(1, 0, 2),
        "w2": w2_rows, "b1": b1_cols,
        "ln_g": np.asarray(L0_ffn_ln_g).T, "ln_b": np.asarray(L0_ffn_ln_b).T,
        "gw": np.asarray(L0_attn_W_qkv),
        "qk_gain": np.broadcast_to(gain[None], (P,) + gain.shape),
        "ident": np.eye(P, dtype=f), "masks": masks, "cos": cos, "sin": sin,
    }
    arrays = {k: np.ascontiguousarray(a) for k, a in arrays.items()}
    nc = bacc.Bacc("TRN2", target_bir_lowering=False, num_devices=1)
    aps = {k: nc.dram_tensor(f"in_{k}", a.shape, mybir.dt.float32, kind="ExternalInput").ap() for k, a in arrays.items()}
    out = nc.dram_tensor("out_x", (SEQS, N_TOK, D), mybir.dt.float32, kind="ExternalOutput").ap()
    build(nc, aps["x"], out, aps)
    r = run_bass_kernel_spmd(nc, [{f"in_{k}": a for k, a in arrays.items()}], core_ids=[0])
    return r.results[0]["out_x"]
```

```python
import numpy as np

import concourse.bass as bass
from concourse import mybir
from contextlib import ExitStack

SEQS, N_TOK, D = 4, 1024, 128
P = 128
TILES = N_TOK // P
GROUP = 4
GROUPS = TILES // GROUP
LAYERS = 2
HEADS, HEAD_D, WINDOW = 8, 64, 64
HALF = HEAD_D // 2
INNER = HEADS * HEAD_D
PAIRS = HEADS // 2
HID = int(D * 4 * 2 / 3)
HID_CHUNKS = [(0, 128), (128, 128), (256, HID - 256)]
N_CHUNKS = len(HID_CHUNKS)
B2_ROW = HID - 256
STEPS = 2 * LAYERS * TILES
LN_EPS = 1e-5
NORM2_MIN = 1e-24
MASKED = -1e30
SCORE_SCALE = float(D) ** -0.5
BANKS = 8
PAIR = 2
LOOK = 2
OFFSET = 6
SLOTS = 4
SET_UP = 2 + 4 * LAYERS
ZEROED = 10


def sequence_blocks():
    blocks = []
    for i in range(2):
        groups = range(i * GROUPS, (i + 1) * GROUPS)
        blocks += [[("input_stats", g) for g in groups], [("input_norm", g) for g in groups]]
        first, last = i * LAYERS * TILES, (i + 1) * LAYERS * TILES
        for n in range(first - LOOK, last + 3):
            ff = [n // GROUP - 1 if n % GROUP == k and first < n - k <= last else None for k in range(3)]
            steps = [("transpose_qk", n), ("transpose_probs", n - 1), ("ff_down", ff[2]), ("transpose_x", n + LOOK),
                     ("scores", n), ("ff_stats", ff[1]), ("mix_values", n - 1), ("rope_finish", n + 1),
                     ("probs_finish", n), ("ff_norm", ff[1]), ("project", n + LOOK), ("ff_transpose", ff[1]),
                     ("attend_out", n - 1), ("ff_shift", ff[0]), ("ff_up", ff[1])]
            blocks.append([(stage, m) if m is not None and (stage.startswith("ff_") or first <= m < last) else None
                           for stage, m in steps])
        blocks += [[("pass_out", g)] for g in groups]
        if i == 0:
            blocks += [[("global_stats", 0)], [("global_norm", 0), ("global_stats", 1), ("global_transpose", 0), ("global_project", 0)],
                       [("global_norm", 1), ("global_transpose", 1), ("global_project", 1)]]
            for t in range(TILES + 2):
                steps = [("global_scores", t), ("global_probs", t - 1), ("global_mix", t - 2)]
                blocks.append([(stage, m) if 0 <= m < TILES else None for stage, m in steps])
    return blocks


def stage_order():
    blocks = sequence_blocks()
    order = []
    for i in range(len(blocks) + OFFSET):
        pair = [blocks[i - s * OFFSET] if 0 <= i - s * OFFSET < len(blocks) else [] for s in range(PAIR)]
        for k in range(max(map(len, pair))):
            order += [(block[k][0], s, block[k][1]) for s, block in enumerate(pair) if k < len(block) and block[k]]
    return order


def stage_banks(stage, m):
    if stage == "transpose_x":
        return ["xT"]
    if stage == "project":
        return ["q", "k", "v"]
    if stage == "transpose_qk":
        return ["qT", "kT"]
    if stage == "scores":
        return ["s0", "s1"]
    if stage == "transpose_probs":
        return ["p0", "p1"]
    if stage == "mix_values":
        return ["oT"]
    if stage == "attend_out":
        return ["y"]
    if stage == "ff_transpose":
        return ["ffT"]
    if stage == "ff_up":
        up = []
        for c in range(N_CHUNKS):
            up += [f"gate{c}", f"lin{c}"]
        return up
    if stage == "ff_down":
        return ["ff"]
    if stage == "global_transpose":
        return ["GxT"]
    if stage == "global_project":
        return ["Gq", "Gk", "Gv"]
    if stage == "global_scores":
        return [f"Gs{c}" for c in range(m // GROUP + 1)]
    if stage == "global_probs":
        return [f"Gp{c}" for c in range(m // GROUP + 1)]
    if stage == "global_mix":
        return ["Go"]
    return []


class Sequence:

    def __init__(self, sb, s):
        def own(name, shape):
            return sb(f"{name}{s}", shape, mybir.dt.float32)

        self.s = s
        self.x = own("x", [P, TILES, D])
        self.y = own("y", [P, TILES, D])
        self.hT = own("hT", [P, N_TOK + 1])
        self.v_odd = own("v_odd", [P, SLOTS, INNER])
        self.v_even = own("v_even", [P, SLOTS, INNER])
        self.kT = own("kT", [P, PAIRS, WINDOW + SLOTS * P])
        self.qT = own("qT", [P, PAIRS, P])
        self.squares = own("squares", [P, 2 * INNER])
        self.norm2 = own("norm2", [P, 2 * HEADS])
        self.inv_norm = own("inv_norm", [P, 2 * HEADS])
        self.rope_a = own("rope_a", [P, 2 * INNER])
        self.rope_b = own("rope_b", [P, 2 * INNER])
        self.roped = own("roped", [P, 2 * INNER])
        self.neg_max = own("neg_max", [P, HEADS])
        self.row_sum = own("row_sum", [P, HEADS])
        self.inv_sum = own("inv_sum", [P, HEADS])
        self.probs = own("probs", [P, HEADS, P])
        self.pT = own("pT", [P, HEADS, P])
        self.oT = own("oT", [P, PAIRS, P])
        self.shifted = own("shifted", [P, TILES, D])
        self.stats = own("stats", [P, GROUP, 6])
        self.mean_var = own("mean_var", [P, 2, GROUP, 2])
        self.var_eps = own("var_eps", [P, 2, GROUP])
        self.rstd = own("rstd", [P, 2, GROUP])
        self.normed = own("normed", [P, GROUP, D])
        self.nT = own("nT", [P, GROUP * P])
        self.g_kT = self.v_odd[:, 0:2, :].rearrange("p a b -> p (a b)")
        self.g_v = self.v_odd[:, 2:4, :].rearrange("p a b -> p (a b)").rearrange("p (t d) -> p t d", d=D)
        self.g_qT = self.v_even[:, 0:2, :].rearrange("p a b -> p (a b)")
        self.g_probs = [self.probs, self.rope_a[:, :].rearrange("p (a b) -> p a b", b=P)]
        self.g_pT = [self.pT, self.rope_b[:, :].rearrange("p (a b) -> p a b", b=P)]
        self.g_max = own("g_max", [P, 2, 2])
        self.g_negmax = own("g_negmax", [P, 2])
        self.g_sum = own("g_sum", [P, 2, 2])
        self.g_total = own("g_total", [P, 2])
        self.g_inv = own("g_inv", [P, 2])

    def add_semaphores(self, sem):
        def own(name):
            return sem(f"{name}{self.s}")

        self.x_loaded = own("x_loaded")
        self.hT_ready = own("hT_ready")
        self.squares_ready = own("squares_ready")
        self.norm2_ready = own("norm2_ready")
        self.norm2_clipped = own("norm2_clipped")
        self.inv_norm_ready = own("inv_norm_ready")
        self.products_ready = own("products_ready")
        self.rope_sum_ready = own("rope_sum_ready")
        self.roped_ready = own("roped_ready")
        self.qT_ready = own("qT_ready")
        self.kT_ready = own("kT_ready")
        self.v_ready = own("v_ready")
        self.v_shifted = [own(f"v_shifted{i}_") for i in range(SLOTS)]
        self.max_ready = own("max_ready")
        self.exp_ready = own("exp_ready")
        self.inv_sum_ready = own("inv_sum_ready")
        self.probs_ready = own("probs_ready")
        self.pT_ready = own("pT_ready")
        self.oT_ready = own("oT_ready")
        self.attended = own("attended")
        self.y_shifted = own("y_shifted")
        self.stats_ready = own("stats_ready")
        self.mean_var_ready = own("mean_var_ready")
        self.eps_added = own("eps_added")
        self.rstd_ready = own("rstd_ready")
        self.normed_ready = own("normed_ready")
        self.nT_ready = own("nT_ready")
        self.ff_added = own("ff_added")
        self.x_updated = own("x_updated")
        self.gqkv_ready = own("gqkv_ready")
        self.gmax_part = own("gmax_part")
        self.gmax_ready = own("gmax_ready")
        self.gexp_ready = own("gexp_ready")
        self.gtotal_ready = own("gtotal_ready")
        self.ginv_ready = own("ginv_ready")
        self.gpT_ready = own("gpT_ready")
        self.g_added = own("g_added")
        self.stored = own("stored")


def build(nc, x_in, out, w):
    fp32, bf16 = mybir.dt.float32, mybir.dt.bfloat16
    ALU, ACT, AX = mybir.AluOpType, mybir.ActivationFunctionType, mybir.AxisListType
    ORDER = stage_order()

    fills = [(what, s, m) for stage, s, m in ORDER for what in stage_banks(stage, m)]
    fill = {f: k for k, f in enumerate(fills)}

    ctx = ExitStack()
    with ctx:
        def sb(name, shape, dt=fp32):
            return ctx.enter_context(nc.sbuf_tensor(name, shape, dt))

        first_sem = []

        def sem(name):
            s = ctx.enter_context(nc.semaphore(name))
            first_sem.append(s)
            return s

        wqkv = sb("wqkv", [P, LAYERS, 3 * INNER])
        wo = sb("wo", [P, LAYERS, PAIRS, D])
        w1 = sb("w1", [P, LAYERS, 2 * HID])
        w2 = sb("w2", [P, LAYERS, N_CHUNKS, D])
        b1 = sb("b1", [P, LAYERS, 2, N_CHUNKS])
        ln_g = sb("ln_g", [P, LAYERS])
        ln_b = sb("ln_b", [P, LAYERS])
        gw = sb("gw", [P, 3 * D])
        ident = sb("ident", [P, P])
        ident16 = sb("ident16", [P, P], bf16)
        mask16 = sb("mask16", [P, 2 * 4 * P + P], bf16)
        window_mask = mask16[:, 0:512]
        first_mask = mask16[:, 512:1024]
        causal_mask = mask16[:, 1024:1152]
        cos_t = sb("cos_t", [P, LAYERS, TILES, 2, HEAD_D])
        sin_t = sb("sin_t", [P, LAYERS, TILES, 2, HEAD_D])
        minus_half = sb("minus_half", [P, 2 * HEADS])

        gate = sb("gate", [P, 2, GROUP * P])
        hid = sb("hid", [P, N_CHUNKS, GROUP * P])
        seqs = [Sequence(sb, s) for s in range(PAIR)]
        q0 = seqs[0]
        cos_raw = q0.v_odd[:, 0:2, :].rearrange("p a b -> p (a b)").rearrange("p (t j d) -> p t j d", t=TILES, j=2)
        sin_raw = q0.v_odd[:, 2:4, :].rearrange("p a b -> p (a b)").rearrange("p (t j d) -> p t j d", t=TILES, j=2)
        mask_f = q0.v_even[:, :, :].rearrange("p a b -> p (a b)")[:, 0:2 * 4 * P + P]
        qk_gain = q0.squares[:, 0:LAYERS * 4 * HEAD_D].rearrange("p (l a b d) -> p l a b d", l=LAYERS, a=2, b=2)

        banks = [ctx.enter_context(nc.psum_tensor(f"bank{i}", [P, 512], fp32)) for i in range(BANKS)]

        loaded = sem("loaded")
        set_up = sem("set_up")
        zeroed = sem("zeroed")
        seq_done = sem("seq_done")
        seq_idle = sem("seq_idle")
        seq_go = sem("seq_go")
        cleared_from = len(first_sem)

        full = [sem(f"full{b}") for b in range(BANKS)]
        gate_ready = sem("gate_ready")
        hid_ready = sem("hid_ready")
        for q in seqs:
            q.add_semaphores(sem)
        cleared = [s.num for s in first_sem[cleared_from:]]
        assert cleared == list(range(cleared[0], cleared[0] + len(cleared)))

        def pass_of(n):
            return n // (LAYERS * TILES)

        def layer_of(n):
            return n // TILES % LAYERS

        ln_no, through_no, ff_no = {}, {}, {}
        for stage, s, m in ORDER:
            if stage in ("input_stats", "ff_stats", "global_stats"):
                ln_no[stage, s, m] = sum(key[1] == s for key in ln_no)
            if stage in ("ff_norm", "global_norm"):
                through_no[stage, s, m] = sum(key[1] == s for key in through_no)
            if stage == "ff_up":
                ff_no[s, m] = len(ff_no)
        ff_stages = [(stage, s, m) for stage, s, m in ORDER if stage in ("ff_up", "ff_down")]
        assert all(up[1:] == down[1:] for up, down in zip(ff_stages[::2], ff_stages[1::2]))
        g_unit = {}
        for t in range(TILES):
            for c in range(t // GROUP + 1):
                g_unit[t, c] = len(g_unit) + 1

        def read_by(what, s, m):
            q = seqs[s]
            c = int(what[-1]) if what[-1].isdigit() else 0
            kind = what.rstrip("0123456789")
            if kind in ("gate", "lin"):
                return (gate_ready if kind == "gate" else hid_ready, N_CHUNKS * ff_no[s, m] + c + 1)
            if kind in ("Gs", "Gp"):
                return (q.gexp_ready if kind == "Gs" else q.gpT_ready, g_unit[m, c])
            if kind in ("ffT", "GxT"):
                return q.nT_ready, through_no["ff_norm" if kind == "ffT" else "global_norm", s, m] + 1
            return {
                "xT": (q.hT_ready, 2 * m + 2),
                "q": (q.products_ready, 6 * m + 3),
                "k": (q.products_ready, 6 * m + 6),
                "v": (q.v_ready, m + 1),
                "qT": (q.qT_ready, m + 1),
                "kT": (q.kT_ready, m + 1),
                "s": (q.exp_ready, 2 * m + c + 1),
                "p": (q.pT_ready, 2 * m + c + 1),
                "oT": (q.oT_ready, m + 1),
                "y": (q.attended, m + 1),
                "ff": (q.ff_added, m + 1),
                "Gq": (q.gqkv_ready, 3 * m + 1),
                "Gk": (q.gqkv_ready, 3 * m + 2),
                "Gv": (q.gqkv_ready, 3 * m + 3),
                "Go": (q.g_added, m + 1),
            }[kind]

        def bank(what, q, m):
            return banks[fill[what, q.s, m] % BANKS]

        def take_bank(pe, what, q, m):
            k = fill[what, q.s, m]
            if k >= BANKS:
                pe.wait_ge(*read_by(*fills[k - BANKS]))
            return banks[k % BANKS]

        def filled(ins, what, q, m):
            ins.then_inc(full[fill[what, q.s, m] % BANKS], 1)

        def wait_full(eng, what, q, m):
            k = fill[what, q.s, m]
            eng.wait_ge(full[k % BANKS], k // BANKS + 1)
            return banks[k % BANKS]

        def end_sequence(eng, it):
            eng.sem_inc(seq_done, 1)
            eng.wait_ge(seq_go, it + 1)

        block = ctx.enter_context(nc.Block())

        @block.sync
        def _(sp):
            for dst, src in ((ident[:, :], w["ident"]), (wqkv[:, :, :], w["wqkv"]),
                             (cos_raw[:, :, :, :], w["cos"]), (sin_raw[:, :, :, :], w["sin"]),
                             (qk_gain[:, :, :, :, :], w["qk_gain"]), (mask_f[:, :], w["masks"]),
                             (wo[:, :, :, :], w["wo"]), (w1[:, :, :], w["w1"]),
                             (w2[:, :, :, :], w["w2"]), (b1[:, :, :, :], w["b1"]),
                             (ln_g[:, :], w["ln_g"]), (ln_b[:, :], w["ln_b"]), (gw[:, :], w["gw"])):
                sp.dma_start(dst, src).then_inc(loaded, 16)

            with sp.Fori(0, SEQS // PAIR) as it:
                for q in seqs:
                    sp.dma_start(q.x[:, :, :], x_in[bass.ds(PAIR * it + q.s, 1), :, :].rearrange("s (t p) d -> p (s t) d", p=P)).then_inc(q.x_loaded, 16)
                for stage, s, m in ORDER:
                    q = seqs[s]
                    if stage == "project":
                        slot, slot_before = m % SLOTS, (m - 1) % SLOTS
                        sp.wait_ge(q.v_ready, m + 1)
                        if m >= SLOTS:
                            wait_full(sp, "oT", q, m - SLOTS)
                        if m % TILES > 0:
                            sp.dma_start(q.v_even[0:64, slot, :], q.v_odd[64:128, slot_before, :]).then_inc(q.v_shifted[slot], 16)
                        sp.dma_start(q.v_even[64:128, slot, :], q.v_odd[0:64, slot, :]).then_inc(q.v_shifted[slot], 16)
                    if stage == "ff_shift":
                        g = m % GROUPS
                        a = GROUP * g
                        sp.wait_ge(q.attended, GROUP * (m + 1))
                        up = q.shifted[:, :, 64:128]
                        src = q.y[:, :, 64:128]
                        sp.dma_start(q.shifted[:, a:a + GROUP, 0:64], q.y[:, a:a + GROUP, 0:64]).then_inc(q.y_shifted, 16)
                        sp.dma_start(up[16:128, a:a + GROUP, :], src[15:127, a:a + GROUP, :]).then_inc(q.y_shifted, 16)
                        sp.dma_start(up[1:16, a:a + GROUP, :], src[0:15, a:a + GROUP, :]).then_inc(q.y_shifted, 16)
                        last = min(GROUP, TILES - 1 - a)
                        sp.dma_start(up[0:1, a + 1:a + 1 + last, :], src[127:128, a:a + last, :]).then_inc(q.y_shifted, 16)
                    if stage == "pass_out" and m >= GROUPS:
                        g = m % GROUPS
                        sp.wait_ge(q.x_updated, m + 1)
                        sp.dma_start(out[bass.ds(PAIR * it + s, 1), g * 512:(g + 1) * 512, :].rearrange("s (t p) d -> p (s t) d", p=P),
                                     q.x[:, g * GROUP:(g + 1) * GROUP, :]).then_inc(q.stored, 16)
                for q in seqs:
                    sp.wait_ge(q.stored, 16 * GROUPS)
                sp.wait_ge(seq_done, 4 * it + 4)
                sp.sem_inc(seq_idle, 1)
                sp.sem_clear(range(cleared[0], cleared[-1] + 1))
                sp.sem_inc(seq_go, 1)

        @block.tensor
        def _(pe):
            pe.wait_ge(loaded, 16 * 13)
            pe.wait_ge(zeroed, ZEROED)
            pe.wait_ge(set_up, SET_UP)
            with pe.Fori(0, SEQS // PAIR) as it:
                for stage, s, m in ORDER:
                    q = seqs[s]
                    t = m % TILES
                    lay = layer_of(m)
                    if stage == "transpose_x":
                        if lay == 0:
                            pe.wait_ge(q.normed_ready, ln_no["input_stats", s, pass_of(m) * GROUPS + t // GROUP] + 1)
                        else:
                            pe.wait_ge(q.ff_added, m // GROUP - GROUPS + 1)
                        b = take_bank(pe, "xT", q, m)
                        filled(pe.transpose(b[:, 0:P], q.y[:, t, :], ident[:, :]), "xT", q, m)
                    if stage == "project":
                        pe.wait_ge(q.hT_ready, 2 * m + 2)
                        for j, what in enumerate("qkv"):
                            b = take_bank(pe, what, q, m)
                            mm = pe.matmul(b[:, :], q.hT[:, t * P:(t + 1) * P], wqkv[:, lay, j * INNER:(j + 1) * INNER],
                                           start=True, stop=True)
                            filled(mm, what, q, m)
                    if stage == "transpose_qk":
                        pe.wait_ge(q.roped_ready, m + 1)
                        for j, what in enumerate(("qT", "kT")):
                            b = take_bank(pe, what, q, m)
                            for c in range(PAIRS):
                                mm = pe.transpose(b[:, c * P:(c + 1) * P],
                                                  q.roped[:, j * INNER + c * P:j * INNER + (c + 1) * P], ident[:, :])
                            filled(mm, what, q, m)
                    if stage == "scores":
                        pe.wait_ge(q.qT_ready, m + 1)
                        pe.wait_ge(q.kT_ready, m + 1)
                        for win in range(2):
                            b = take_bank(pe, f"s{win}", q, m)
                            mask = first_mask if t == 0 and win == 0 else window_mask
                            pe.matmul(b[:, :], ident16[:, :], mask, start=True, stop=True, skip_group_check=True)
                            k0 = m % SLOTS * P + win * WINDOW
                            for c in range(PAIRS):
                                for h in range(2):
                                    r = slice(64 * h, 64 * h + 64)
                                    mm = pe.matmul(b[r, c * P:(c + 1) * P], q.qT[r, c, win * 64:win * 64 + 64],
                                                   q.kT[r, c, k0:k0 + 2 * WINDOW], start=False, stop=True,
                                                   skip_group_check=True)
                            filled(mm, f"s{win}", q, m)
                    if stage == "transpose_probs":
                        for win in range(2):
                            pe.wait_ge(q.probs_ready, 2 * m + win + 1)
                            b = take_bank(pe, f"p{win}", q, m)
                            for c in range(PAIRS):
                                mm = pe.transpose(b[:, c * P:(c + 1) * P], q.probs[:, win * PAIRS + c, :], ident[:, :])
                            filled(mm, f"p{win}", q, m)
                    if stage == "mix_values":
                        b = take_bank(pe, "oT", q, m)
                        for win in range(2):
                            pe.wait_ge(q.pT_ready, 2 * m + win + 1)
                            if win == 0:
                                same = [i for i in range(m + 1) if i % SLOTS == m % SLOTS]
                                pe.wait_ge(q.v_shifted[m % SLOTS], sum(32 if i % TILES else 16 for i in same))
                            v = (q.v_even, q.v_odd)[win]
                            for c in range(PAIRS):
                                for h in range(2):
                                    head = 2 * c + h
                                    mm = pe.matmul(b[64 * h:64 * h + 64, c * P + win * 64:c * P + win * 64 + 64],
                                                   v[:, m % SLOTS, head * 64:head * 64 + 64],
                                                   q.pT[:, win * PAIRS + c, 64 * h:64 * h + 64],
                                                   start=True, stop=True, skip_group_check=True)
                        filled(mm, "oT", q, m)
                    if stage == "attend_out":
                        pe.wait_ge(q.oT_ready, m + 1)
                        b = take_bank(pe, "y", q, m)
                        for c in range(PAIRS):
                            mm = pe.matmul(b[:, 0:D], q.oT[:, c, :], wo[:, lay, c, :],
                                           start=(c == 0), stop=(c == PAIRS - 1))
                        filled(mm, "y", q, m)
                    if stage in ("ff_up", "ff_down"):
                        lay = m // GROUPS % LAYERS
                    if stage == "ff_transpose":
                        pe.wait_ge(q.normed_ready, ln_no["ff_stats", s, m] + 1)
                        b = take_bank(pe, "ffT", q, m)
                        for i in range(GROUP):
                            mm = pe.transpose(b[:, i * P:(i + 1) * P], q.normed[:, i, :], ident[:, :])
                        filled(mm, "ffT", q, m)
                    if stage == "ff_up":
                        pe.wait_ge(q.nT_ready, through_no["ff_norm", s, m] + 1)
                        for c, (at, size) in enumerate(HID_CHUNKS):
                            for what, base in ((f"gate{c}", HID), (f"lin{c}", 0)):
                                b = take_bank(pe, what, q, m)
                                mm = pe.matmul(b[0:size, :], w1[:, lay, base + at:base + at + size], q.nT[:, :],
                                               start=True, stop=True)
                                filled(mm, what, q, m)
                    if stage == "ff_down":
                        pe.wait_ge(hid_ready, N_CHUNKS * (ff_no[s, m] + 1))
                        b = take_bank(pe, "ff", q, m)
                        for i in range(GROUP):
                            for c, (at, size) in enumerate(HID_CHUNKS):
                                rows = size + 1 if c == N_CHUNKS - 1 else size
                                mm = pe.matmul(b[:, i * P:(i + 1) * P], hid[0:rows, c, i * P:(i + 1) * P],
                                               w2[0:rows, lay, c, :], start=(c == 0), stop=(c == N_CHUNKS - 1))
                        filled(mm, "ff", q, m)
                    if stage == "global_transpose":
                        pe.wait_ge(q.normed_ready, ln_no["global_stats", s, m] + 1)
                        b = take_bank(pe, "GxT", q, m)
                        for i in range(GROUP):
                            mm = pe.transpose(b[:, i * P:(i + 1) * P], q.normed[:, i, :], ident[:, :])
                        filled(mm, "GxT", q, m)
                    if stage == "global_project":
                        pe.wait_ge(q.nT_ready, through_no["global_norm", s, m] + 1)
                        for j, what in enumerate(("Gq", "Gk")):
                            b = take_bank(pe, what, q, m)
                            filled(pe.matmul(b[:, :], gw[:, j * D:(j + 1) * D], q.nT[:, :], start=True, stop=True), what, q, m)
                        b = take_bank(pe, "Gv", q, m)
                        for i in range(GROUP):
                            mm = pe.matmul(b[:, i * P:(i + 1) * P], q.nT[:, i * P:(i + 1) * P], gw[:, 2 * D:3 * D],
                                           start=True, stop=True)
                        filled(mm, "Gv", q, m)
                    if stage == "global_scores":
                        pe.wait_ge(q.gqkv_ready, 3 * (m // GROUP + 1))
                        for c in range(m // GROUP + 1):
                            b = take_bank(pe, f"Gs{c}", q, m)
                            keys = min((c + 1) * 512, (m + 1) * P) - c * 512
                            diagonal = c == m // GROUP
                            mm = pe.matmul(b[:, 0:keys], q.g_qT[:, m * P:(m + 1) * P], q.g_kT[:, c * 512:c * 512 + keys],
                                           start=True, stop=True)
                            if diagonal:
                                mm = pe.matmul(b[:, keys - P:keys], ident16[:, :], causal_mask, start=False, stop=True,
                                               skip_group_check=True)
                            filled(mm, f"Gs{c}", q, m)
                    if stage == "global_probs":
                        for c in range(m // GROUP + 1):
                            pe.wait_ge(q.gexp_ready, g_unit[m, c])
                            b = take_bank(pe, f"Gp{c}", q, m)
                            for j in range(min(GROUP, m + 1 - c * GROUP)):
                                mm = pe.transpose(b[:, j * P:(j + 1) * P], q.g_probs[m % 2][:, c * GROUP + j, :], ident[:, :])
                            filled(mm, f"Gp{c}", q, m)
                    if stage == "global_mix":
                        b = take_bank(pe, "Go", q, m)
                        for j in range(m + 1):
                            if j % GROUP == 0:
                                pe.wait_ge(q.gpT_ready, g_unit[m, j // GROUP])
                            mm = pe.matmul(b[:, 0:D], q.g_pT[m % 2][:, j, :], q.g_v[:, j, :], start=(j == 0), stop=(j == m))
                        filled(mm, "Go", q, m)
                end_sequence(pe, it)

        @block.scalar
        def _(act):
            act.wait_ge(loaded, 16 * 13)
            act.wait_ge(zeroed, ZEROED)
            act.wait_ge(set_up, SET_UP)

            with act.Fori(0, SEQS // PAIR) as it:
                for stage, s, m in ORDER:
                    q = seqs[s]
                    t = m % TILES
                    lay = layer_of(m)
                    if stage == "transpose_x":
                        b = wait_full(act, "xT", q, m)
                        act.activation(q.hT[0:64, t * P:(t + 1) * P], b[0:64, 0:P], ACT.Copy).then_inc(q.hT_ready, 1)
                        ins = act.activation(q.hT[64:128, t * P + 1:(t + 1) * P + 1], b[64:128, 0:P], ACT.Copy)
                        ins.then_inc(q.hT_ready, 1)
                    if stage == "project":
                        if m:
                            act.wait_ge(q.norm2_ready, m)
                        for j, what in enumerate("qk"):
                            b = wait_full(act, what, q, m)
                            ins = act.activation(q.squares[:, j * INNER:(j + 1) * INNER], b[:, :], ACT.Square)
                            ins.then_inc(q.squares_ready, 1)
                        b = wait_full(act, "v", q, m)
                        ins = act.activation(q.v_odd[:, m % SLOTS, :], b[:, :], ACT.Copy)
                        ins.then_inc(q.v_ready, 1)
                    if stage == "transpose_qk":
                        b = wait_full(act, "qT", q, m)
                        ins = act.activation(q.qT[:, :, :], b[:, :].rearrange("p (c q) -> p c q", c=PAIRS), ACT.Copy)
                        ins.then_inc(q.qT_ready, 1)
                        b = wait_full(act, "kT", q, m)
                        kT_new = b[:, :].rearrange("p (c k) -> p c k", c=PAIRS)
                        at = WINDOW + m % SLOTS * P
                        ins = act.activation(q.kT[:, :, at:at + P], kT_new, ACT.Copy)
                        if m % SLOTS == SLOTS - 1:
                            ins = act.activation(q.kT[:, :, 0:WINDOW], kT_new[:, :, WINDOW:P], ACT.Copy)
                        ins.then_inc(q.kT_ready, 1)
                    if stage == "scores":
                        for win in range(2):
                            act.wait_ge(q.max_ready, 2 * m + win + 1)
                            b = bank(f"s{win}", q, m)
                            for c in range(PAIRS):
                                i = win * PAIRS + c
                                ins = act.activation(q.probs[:, i, :], b[:, c * P:(c + 1) * P], ACT.Exp,
                                                     bias=q.neg_max[:, i:i + 1], scale=1.0,
                                                     accum_out=q.row_sum[:, i:i + 1])
                            ins.then_inc(q.exp_ready, 1)
                    if stage == "transpose_probs":
                        for win in range(2):
                            b = wait_full(act, f"p{win}", q, m)
                            act.activation(q.pT[:, win * PAIRS:(win + 1) * PAIRS, :].rearrange("p c r -> p (c r)"), b[:, :],
                                           ACT.Copy).then_inc(q.pT_ready, 1)
                    if stage in ("ff_transpose", "ff_up"):
                        lay = m // GROUPS % LAYERS
                    if stage == "ff_transpose":
                        b = wait_full(act, "ffT", q, m)
                        ins = act.activation(q.nT[:, :], b[:, :], ACT.Identity, bias=ln_b[:, lay:lay + 1], scale=ln_g[:, lay:lay + 1])
                        ins.then_inc(q.nT_ready, 1)
                    if stage == "ff_up":
                        for c, (at, size) in enumerate(HID_CHUNKS):
                            b = wait_full(act, f"gate{c}", q, m)
                            k = N_CHUNKS * ff_no[s, m] + c
                            if k >= 2:
                                act.wait_ge(hid_ready, k - 1)
                            ins = act.activation(gate[0:size, k % 2, :], b[0:size, :], ACT.Gelu, bias=b1[0:size, lay, 1, c:c + 1])
                            ins.then_inc(gate_ready, 1)
                    if stage == "global_transpose":
                        b = wait_full(act, "GxT", q, m)
                        ins = act.activation(q.nT[:, :], b[:, :], ACT.Copy)
                        ins.then_inc(q.nT_ready, 1)
                    if stage == "global_project":
                        a = m * GROUP
                        for what, dst in (("Gq", q.g_qT[:, a * P:a * P + 512]), ("Gk", q.g_kT[:, a * P:a * P + 512]),
                                          ("Gv", q.g_v[:, a:a + GROUP, :].rearrange("p t d -> p (t d)"))):
                            b = wait_full(act, what, q, m)
                            ins = act.activation(dst, b[:, :], ACT.Copy)
                            ins.then_inc(q.gqkv_ready, 1)
                    if stage == "global_scores":
                        act.wait_ge(q.gmax_ready, m + 1)
                        for c in range(m // GROUP + 1):
                            b = bank(f"Gs{c}", q, m)
                            keys = min((c + 1) * 512, (m + 1) * P) - c * 512
                            ins = act.activation(q.g_probs[m % 2][:, c * GROUP:c * GROUP + keys // P, :].rearrange("p a b -> p (a b)"),
                                                 b[:, 0:keys], ACT.Exp, bias=q.g_negmax[:, m % 2:m % 2 + 1], scale=SCORE_SCALE,
                                                 accum_out=q.g_sum[:, m % 2, c:c + 1])
                            ins.then_inc(q.gexp_ready, 1)
                end_sequence(act, it)

        @block.vector
        def _(dve):
            dve.wait_ge(loaded, 16 * 13)
            dve.tensor_copy(ident16[:, :], ident[:, :]).then_inc(set_up, 1)
            dve.tensor_copy(mask16[:, :], mask_f[:, :]).then_inc(set_up, 1)
            for lay in range(LAYERS):
                for raw, table, j in ((cos_raw, cos_t, 0), (sin_raw, sin_t, 1)):
                    for i in range(2):
                        gain = qk_gain[:, lay, j, i, :].unsqueeze(1).to_broadcast([P, TILES, HEAD_D])
                        dve.tensor_tensor(table[:, lay, :, i, :], raw[:, :, i, :], gain, ALU.mult).then_inc(set_up, 1)
            dve.wait_ge(set_up, SET_UP)
            dve.wait_ge(zeroed, ZEROED)

            def token_stats(q, unit, src):
                if unit:
                    dve.wait_ge(q.mean_var_ready, GROUP * unit)
                for i in range(GROUP):
                    dve.bn_stats(q.stats[:, i, :], src[:, i, :]).then_inc(q.stats_ready, 1)
                dve.wait_ge(q.stats_ready, GROUP * (unit + 1))
                for i in range(GROUP):
                    dve.bn_aggr(q.mean_var[:, unit % 2, i, :], q.stats[:, i, :]).then_inc(q.mean_var_ready, 1)

            def normalise(q, unit, src, dst):
                dve.wait_ge(q.rstd_ready, unit + 1)
                for i in range(GROUP):
                    ins = dve.tensor_scalar(dst[:, i, :], src[:, i, :], q.mean_var[:, unit % 2, i, 0:1], q.rstd[:, unit % 2, i:i + 1],
                                            ALU.subtract, ALU.mult)
                ins.then_inc(q.normed_ready, 1)

            with dve.Fori(0, SEQS // PAIR) as it:
                for stage, s, m in ORDER:
                    q = seqs[s]
                    t = m % TILES
                    lay = layer_of(m)
                    a = m % GROUPS * GROUP
                    if stage == "input_stats":
                        if m == 0:
                            dve.wait_ge(q.x_loaded, 16)
                        if m >= GROUPS:
                            dve.wait_ge(q.g_added, a + GROUP)
                        token_stats(q, ln_no[stage, s, m], q.x[:, a:a + GROUP, :])
                    if stage == "input_norm":
                        normalise(q, ln_no["input_stats", s, m], q.x[:, a:a + GROUP, :], q.y[:, a:a + GROUP, :])
                    if stage == "project":
                        if m:
                            dve.wait_ge(q.roped_ready, m)
                        for j, what in enumerate("qk"):
                            dve.wait_ge(q.squares_ready, 2 * m + j + 1)
                            b = bank(what, q, m)
                            a_out = q.rope_a[:, j * INNER:(j + 1) * INNER]
                            b_out = q.rope_b[:, j * INNER:(j + 1) * INNER]
                            cos = cos_t[:, lay, t, j, :].unsqueeze(1).to_broadcast([P, HEADS, HEAD_D])
                            dve.tensor_tensor(a_out.rearrange("p (h d) -> p h d", h=HEADS),
                                              b[:, :].rearrange("p (h d) -> p h d", h=HEADS), cos, ALU.mult).then_inc(q.products_ready, 1)
                            for half in range(2):
                                o, i = half * HALF, (1 - half) * HALF
                                sin = sin_t[:, lay, t, j, o:o + HALF].unsqueeze(1).to_broadcast([P, HEADS, HALF])
                                ins = dve.tensor_tensor(b_out.rearrange("p (h d) -> p h d", h=HEADS)[:, :, o:o + HALF],
                                                        b[:, :].rearrange("p (h d) -> p h d", h=HEADS)[:, :, i:i + HALF],
                                                        sin, ALU.mult)
                                ins.then_inc(q.products_ready, 1)
                        dve.tensor_reduce(q.norm2[:, :], q.squares[:, :].rearrange("p (h d) -> p h d", d=HEAD_D),
                                          AX.X, ALU.add).then_inc(q.norm2_ready, 1)
                    if stage == "rope_finish":
                        dve.wait_ge(q.rope_sum_ready, m + 1)
                        dve.wait_ge(q.inv_norm_ready, m + 1)
                        if m:
                            wait_full(dve, "kT", q, m - 1)
                        inv = q.inv_norm[:, :].unsqueeze(2).to_broadcast([P, 2 * HEADS, HEAD_D])
                        dve.tensor_tensor(q.roped[:, :].rearrange("p (h d) -> p h d", d=HEAD_D),
                                          q.rope_a[:, :].rearrange("p (h d) -> p h d", d=HEAD_D), inv,
                                          ALU.mult).then_inc(q.roped_ready, 1)
                    if stage == "scores":
                        for win in range(2):
                            b = wait_full(dve, f"s{win}", q, m)
                            dve.tensor_reduce(q.neg_max[:, win * PAIRS:(win + 1) * PAIRS],
                                              b[:, :].rearrange("p (c k) -> p c k", c=PAIRS), AX.X, ALU.max,
                                              negate=True).then_inc(q.max_ready, 1)
                    if stage == "probs_finish":
                        for win in range(2):
                            dve.wait_ge(q.exp_ready, 2 * m + win + 1)
                            dve.reciprocal(q.inv_sum[:, win * PAIRS:(win + 1) * PAIRS],
                                           q.row_sum[:, win * PAIRS:(win + 1) * PAIRS]).then_inc(q.inv_sum_ready, 1)
                    if stage == "mix_values":
                        b = wait_full(dve, "oT", q, m)
                        ins = dve.tensor_copy(q.oT[:, :, :], b[:, :].rearrange("p (c q) -> p c q", c=PAIRS))
                        ins.then_inc(q.oT_ready, 1)
                    if stage == "attend_out":
                        b = wait_full(dve, "y", q, m)
                        ins = dve.tensor_tensor(q.y[:, t, :], b[:, 0:D], q.y[:, t, :], ALU.add)
                        ins.then_inc(q.attended, 1)
                    if stage == "ff_stats":
                        dve.wait_ge(q.y_shifted, 4 * 16 * (m + 1))
                        token_stats(q, ln_no[stage, s, m], q.shifted[:, a:a + GROUP, :])
                    if stage in ("ff_norm", "global_norm"):
                        if through_no[stage, s, m]:
                            dve.wait_ge(q.nT_ready, through_no[stage, s, m])
                    if stage == "ff_norm":
                        normalise(q, ln_no["ff_stats", s, m], q.shifted[:, a:a + GROUP, :], q.normed[:, :, :])
                    if stage == "ff_up":
                        lay = m // GROUPS % LAYERS
                        for c, (at, size) in enumerate(HID_CHUNKS):
                            b = wait_full(dve, f"lin{c}", q, m)
                            k = N_CHUNKS * ff_no[s, m] + c
                            dve.wait_ge(gate_ready, k + 1)
                            ins = dve.scalar_tensor_tensor(hid[0:size, c, :], b[0:size, :], b1[0:size, lay, 0, c:c + 1],
                                                           gate[0:size, k % 2, :], ALU.add, ALU.mult)
                            ins.then_inc(hid_ready, 1)
                    if stage == "ff_down":
                        a = m % GROUPS * GROUP
                        b = wait_full(dve, "ff", q, m)
                        rows = q.y[:, a:a + GROUP, :].rearrange("p t d -> p (t d)")
                        ins = dve.tensor_tensor(rows, b[:, :], rows, ALU.add)
                        ins.then_inc(q.ff_added, 1)
                    if stage == "pass_out":
                        g = m % GROUPS
                        i = m // GROUPS
                        dve.wait_ge(q.ff_added, (i * LAYERS + LAYERS - 1) * GROUPS + g + 1)
                        rows = slice(g * GROUP, (g + 1) * GROUP)
                        dve.scalar_tensor_tensor(q.x[:, rows, :].rearrange("p t d -> p (t d)"),
                                                 q.y[:, rows, :].rearrange("p t d -> p (t d)"), 0.5,
                                                 q.x[:, rows, :].rearrange("p t d -> p (t d)"),
                                                 ALU.mult, ALU.add).then_inc(q.x_updated, 1)
                    if stage == "global_stats":
                        dve.wait_ge(q.x_updated, m + 1)
                        token_stats(q, ln_no[stage, s, m], q.x[:, a:a + GROUP, :])
                    if stage == "global_norm":
                        normalise(q, ln_no["global_stats", s, m], q.x[:, a:a + GROUP, :], q.normed[:, :, :])
                    if stage == "global_scores":
                        for c in range(m // GROUP + 1):
                            b = wait_full(dve, f"Gs{c}", q, m)
                            keys = min((c + 1) * 512, (m + 1) * P) - c * 512
                            dve.tensor_reduce(q.g_max[:, m % 2, c:c + 1], b[:, 0:keys], AX.X, ALU.max).then_inc(q.gmax_part, 1)
                        dve.wait_ge(q.gmax_part, g_unit[m, m // GROUP])
                        if m < GROUP:
                            ins = dve.tensor_scalar(q.g_negmax[:, m % 2:m % 2 + 1], q.g_max[:, m % 2, 0:1], -SCORE_SCALE, None, ALU.mult)
                        else:
                            ins = dve.tensor_scalar(q.g_negmax[:, m % 2:m % 2 + 1], q.g_max[:, m % 2, 0:1],
                                                    q.g_max[:, m % 2, 1:2], -SCORE_SCALE, ALU.max, ALU.mult)
                        ins.then_inc(q.gmax_ready, 1)
                    if stage == "global_probs":
                        for c in range(m // GROUP + 1):
                            b = wait_full(dve, f"Gp{c}", q, m)
                            tiles = min(GROUP, m + 1 - c * GROUP)
                            ins = dve.tensor_copy(q.g_pT[m % 2][:, c * GROUP:c * GROUP + tiles, :].rearrange("p a b -> p (a b)"),
                                                  b[:, 0:tiles * P])
                            ins.then_inc(q.gpT_ready, 1)
                        dve.wait_ge(q.gexp_ready, g_unit[m, m // GROUP])
                        total = q.g_sum[:, m % 2, 0:1]
                        if m >= GROUP:
                            total = q.g_total[:, m % 2:m % 2 + 1]
                            dve.tensor_tensor(total, q.g_sum[:, m % 2, 0:1], q.g_sum[:, m % 2, 1:2], ALU.add).then_inc(q.gtotal_ready, 1)
                            dve.wait_ge(q.gtotal_ready, m - GROUP + 1)
                        if m >= 2:
                            dve.wait_ge(q.g_added, m - 1)
                        dve.reciprocal(q.g_inv[:, m % 2:m % 2 + 1], total).then_inc(q.ginv_ready, 1)
                    if stage == "global_mix":
                        b = wait_full(dve, "Go", q, m)
                        dve.wait_ge(q.ginv_ready, m + 1)
                        ins = dve.scalar_tensor_tensor(q.x[:, m, :], b[:, 0:D], q.g_inv[:, m % 2:m % 2 + 1], q.x[:, m, :],
                                                       ALU.mult, ALU.add)
                        ins.then_inc(q.g_added, 1)
                end_sequence(dve, it)

        @block.gpsimd
        def _(pool):
            pool.wait_ge(set_up, SET_UP)
            parts = [(hid[64:128, N_CHUNKS - 1, :], 1.0),
                     (minus_half[:, :], -0.5)]
            for q in seqs:
                parts += [(q.hT[64:128, 0:1], 0.0),
                          (q.kT[:, :, 0:WINDOW], 0.0),
                          (q.v_even[0:64, 0, :], 0.0),
                          (q.shifted[0:1, 0, 64:128], 0.0)]
            assert len(parts) == ZEROED
            for i, (part, value) in enumerate(parts):
                if i:
                    pool.wait_ge(zeroed, i)
                pool.memset(part, value).then_inc(zeroed, 1)
            pool.wait_ge(zeroed, ZEROED)
            with pool.Fori(0, SEQS // PAIR) as it:
                for stage, s, m in ORDER:
                    q = seqs[s]
                    if stage == "project":
                        pool.wait_ge(q.norm2_ready, m + 1)
                        if m:
                            pool.wait_ge(q.roped_ready, m)
                        pool.tensor_scalar(q.inv_norm[:, :], q.norm2[:, :], NORM2_MIN, None, ALU.max).then_inc(q.norm2_clipped, 1)
                        pool.wait_ge(q.norm2_clipped, m + 1)
                        pool.tensor_tensor(q.inv_norm[:, :], q.inv_norm[:, :], minus_half[:, :], ALU.pow).then_inc(q.inv_norm_ready, 1)
                        pool.wait_ge(q.products_ready, 6 * (m + 1))
                        pool.tensor_tensor(q.rope_a[:, :], q.rope_a[:, :], q.rope_b[:, :], ALU.add).then_inc(q.rope_sum_ready, 1)
                    if stage == "probs_finish":
                        for win in range(2):
                            pool.wait_ge(q.inv_sum_ready, 2 * m + win + 1)
                            p = q.probs[:, win * PAIRS:(win + 1) * PAIRS, :]
                            inv = q.inv_sum[:, win * PAIRS:(win + 1) * PAIRS].unsqueeze(2).to_broadcast([P, PAIRS, P])
                            pool.tensor_tensor(p, p, inv, ALU.mult).then_inc(q.probs_ready, 1)
                    if (stage, s, m) in ln_no:
                        u = ln_no[stage, s, m]
                        pool.wait_ge(q.mean_var_ready, GROUP * (u + 1))
                        pool.tensor_scalar(q.var_eps[:, u % 2, :], q.mean_var[:, u % 2, :, 1], LN_EPS, None, ALU.add).then_inc(q.eps_added, 1)
                        pool.wait_ge(q.eps_added, u + 1)
                        if u >= 2:
                            pool.wait_ge(q.normed_ready, u - 1)
                        pool.tensor_tensor(q.rstd[:, u % 2, :], q.var_eps[:, u % 2, :], minus_half[:, 0:GROUP], ALU.pow).then_inc(q.rstd_ready, 1)
                end_sequence(pool, it)


def kernel(L0_attn_x, L0_attn_W_qkv, L0_ffn_wqkv, L0_ffn_q_scale, L0_ffn_k_scale, L0_ffn_wo, L0_ffn_ln_g,
           L0_ffn_ln_b, L0_ffn_w1, L0_ffn_b1, L0_ffn_w2, L0_ffn_b2):
    import concourse.bacc as bacc
    from concourse.bass_utils import run_bass_kernel_spmd

    f = np.float32
    half_idx = np.arange(0, HEAD_D, 2, dtype=f)
    inv_freq = (f(1.0) / f(10000.0) ** (half_idx / f(HEAD_D))).astype(f)
    pos = np.arange(N_TOK, dtype=f)
    angle = pos[:, None] * inv_freq[None, :]
    base = ((half_idx + f(0.4 * HEAD_D)) / f(1.4 * HEAD_D)).astype(f)
    xpos = base[None, :] ** ((pos - N_TOK // 2) / f(WINDOW // 2))[:, None]
    angle, xpos = (np.concatenate([a, a], axis=1) for a in (angle, xpos))
    sign = np.where(np.arange(HEAD_D) < HALF, f(-1), f(1))
    qk_scale = f(8.0)
    cos = np.stack([qk_scale * np.cos(angle) * xpos, np.cos(angle) / xpos], axis=1)
    sin = np.stack([qk_scale * np.sin(angle) * xpos * sign, np.sin(angle) / xpos * sign], axis=1)
    cos, sin = (np.ascontiguousarray(a.reshape(TILES, P, 2, HEAD_D).transpose(1, 0, 2, 3).astype(f)) for a in (cos, sin))
    i, j = np.arange(P)[:, None] % WINDOW, np.arange(P)[None, :]
    inside = (j >= i) & (j <= i + WINDOW)
    window = np.where(inside, f(0), f(MASKED))
    first = np.where(inside & (j >= WINDOW), f(0), f(MASKED))
    causal = np.where(j <= np.arange(P)[:, None], f(0), f(MASKED))
    masks = np.concatenate([np.tile(window, (1, 4)), np.tile(first, (1, 4)), causal], axis=1).astype(f)

    def swap(a):
        return np.concatenate([a[:, HALF:], a[:, :HALF]], axis=1)

    qs, ks = np.asarray(L0_ffn_q_scale), np.asarray(L0_ffn_k_scale)
    gain = np.stack([np.stack([qs, ks], axis=1), np.stack([swap(qs), swap(ks)], axis=1)], axis=1)
    b1 = np.asarray(L0_ffn_b1)
    b1_cols = np.zeros((P, LAYERS, 2, N_CHUNKS), f)
    w2 = np.asarray(L0_ffn_w2)
    w2_rows = np.zeros((P, LAYERS, N_CHUNKS, D), f)
    for c, (at, size) in enumerate(HID_CHUNKS):
        for part in range(2):
            b1_cols[:size, :, part, c] = b1[:, part * HID + at:part * HID + at + size].T
        w2_rows[:size, :, c, :] = w2[:, at:at + size, :].transpose(1, 0, 2)
    w2_rows[B2_ROW, :, N_CHUNKS - 1, :] = np.asarray(L0_ffn_b2)
    arrays = {
        "x": np.asarray(L0_attn_x),
        "wqkv": np.asarray(L0_ffn_wqkv).transpose(1, 0, 2),
        "wo": np.asarray(L0_ffn_wo).reshape(LAYERS, PAIRS, P, D).transpose(2, 0, 1, 3),
        "w1": np.asarray(L0_ffn_w1).transpose(1, 0, 2),
        "w2": w2_rows, "b1": b1_cols,
        "ln_g": np.asarray(L0_ffn_ln_g).T, "ln_b": np.asarray(L0_ffn_ln_b).T,
        "gw": np.asarray(L0_attn_W_qkv),
        "qk_gain": np.broadcast_to(gain[None], (P,) + gain.shape),
        "ident": np.eye(P, dtype=f), "masks": masks, "cos": cos, "sin": sin,
    }
    arrays = {k: np.ascontiguousarray(a) for k, a in arrays.items()}
    nc = bacc.Bacc("TRN2", target_bir_lowering=False, num_devices=1)
    aps = {k: nc.dram_tensor(f"in_{k}", a.shape, mybir.dt.float32, kind="ExternalInput").ap() for k, a in arrays.items()}
    out = nc.dram_tensor("out_x", (SEQS, N_TOK, D), mybir.dt.float32, kind="ExternalOutput").ap()
    build(nc, aps["x"], out, aps)
    r = run_bass_kernel_spmd(nc, [{f"in_{k}": a for k, a in arrays.items()}], core_ids=[0])
    return r.results[0]["out_x"]
```

```python
import numpy as np

import concourse.bass as bass
from concourse import mybir
from contextlib import ExitStack

SEQS, N_TOK, D = 4, 1024, 128
P = 128
TILES = N_TOK // P
GROUP = 4
GROUPS = TILES // GROUP
LAYERS = 2
HEADS, HEAD_D, WINDOW = 8, 64, 64
HALF = HEAD_D // 2
INNER = HEADS * HEAD_D
PAIRS = HEADS // 2
HID = int(D * 4 * 2 / 3)
HID_CHUNKS = [(0, 128), (128, 128), (256, HID - 256)]
N_CHUNKS = len(HID_CHUNKS)
B2_ROW = HID - 256
LN_EPS = 1e-5
NORM2_MIN = 1e-24
MASKED = -1e30
SCORE_SCALE = float(D) ** -0.5
BANKS = 8
PAIR = 2
LOOK = 2
OFFSET = 1
SLOTS = 4
K_SLOTS = 2
W1_COLS = HID + N_CHUNKS * P
SET_UP = 2 + 6 * LAYERS
LOADS = 6
ZEROED = 13


def sequence_blocks():
    blocks = []
    for i in range(2):
        g0, g1 = groups = range(i * GROUPS, (i + 1) * GROUPS)
        if i == 0:
            blocks.append([("input_stats", g0), ("input_norm", g0)])
        first, last = i * LAYERS * TILES, (i + 1) * LAYERS * TILES
        for n in range(first - LOOK, last + 3):
            ff = [n // GROUP - 1 if n % GROUP == k and first < n - k <= last else None for k in range(3)]
            steps = [("ff_stats", ff[1]), ("transpose_qk", n), ("ff_down", ff[2]), ("transpose_probs", n - 1),
                     ("transpose_x", n + LOOK), ("scores", n), ("ff_norm", ff[1]), ("rope_finish", n + 1),
                     ("probs_finish", n), ("mix_values", n - 1), ("ff_transpose", ff[1]), ("project", n + LOOK),
                     ("attend_out", n - 1), ("ff_shift", ff[0]), ("ff_up", ff[1]), ("norm_sums", n + LOOK)]
            block = [(stage, m) if m is not None and (stage.startswith("ff_") or first <= m < last) else None
                     for stage, m in steps]
            if n == first - LOOK and i == 0:
                block += [("input_stats", g1)]
            if n == first - LOOK + 1:
                block += [("input_norm", g1)]
            if n == last - 1:
                block += [("pass_out", g0)]
            if n == last + 1 and i == 0:
                block += [("global_stats", 0)]
            if n == last + 2:
                block += [("pass_out", g1)]
                if i == 0:
                    block += [("global_norm", 0), ("global_stats", 1)]
            blocks.append(block)
        if i == 0:
            blocks.append([None] * 5 + [("global_transpose", 0)] + [None] * 3 + [("global_norm", 1)] + [None] * 3
                          + [("global_project", 0)])
            for t in range(TILES + 2):
                steps = [("global_scores", t), (None, None), ("global_probs", t - 1), (None, None), ("global_mix", t - 2)]
                block = [(stage, m) if stage and 0 <= m < TILES else None for stage, m in steps]
                if t == 0:
                    block = [("global_transpose", 1), ("global_scores", 0), ("global_project", 1)]
                if t == GROUP + 2:
                    block += [("input_stats", GROUPS)]
                if t == GROUP + 3:
                    block += [("input_norm", GROUPS)]
                if t == TILES + 1:
                    block += [("input_stats", GROUPS + 1)]
                blocks.append(block)
    return blocks


def stage_order():
    blocks = sequence_blocks()
    order = []
    for i in range(len(blocks) + OFFSET):
        pair = [blocks[i - s * OFFSET] if 0 <= i - s * OFFSET < len(blocks) else [] for s in range(PAIR)]
        for k in range(max(map(len, pair))):
            order += [(block[k][0], s, block[k][1]) for s, block in enumerate(pair) if k < len(block) and block[k]]
    return order


def stage_banks(stage, m):
    if stage == "transpose_x":
        return ["xT"]
    if stage == "project":
        return ["q", "k", "v"]
    if stage == "transpose_qk":
        return ["qT", "kT"]
    if stage == "scores":
        return ["s0", "s1"]
    if stage == "transpose_probs":
        return ["p0", "p1"]
    if stage == "mix_values":
        return ["oT"]
    if stage == "attend_out":
        return ["y"]
    if stage == "ff_transpose":
        return ["ffT"]
    if stage == "ff_up":
        up = []
        for c in range(N_CHUNKS):
            up += [f"gate{c}", f"lin{c}"]
        return up
    if stage == "ff_down":
        return ["ff"]
    if stage == "global_transpose":
        return ["GxT"]
    if stage == "global_project":
        return ["Gq", "Gk", "Gv"]
    if stage == "global_scores":
        return [f"Gs{c}" for c in range(m // GROUP + 1)]
    if stage == "global_probs":
        return [f"Gp{c}" for c in range(m // GROUP + 1)]
    if stage == "global_mix":
        return ["Go"]
    return []


class Sequence:

    def __init__(self, sb, s):
        def own(name, shape):
            return sb(f"{name}{s}", shape, mybir.dt.float32)

        self.s = s
        self.x = own("x", [P, TILES, D])
        self.y = own("y", [P, TILES, D])
        self.hT_hi = sb(f"hT_hi{s}", [P, K_SLOTS * P + 1], mybir.dt.float32r)
        self.hT_lo = sb(f"hT_lo{s}", [P, K_SLOTS * P + 1], mybir.dt.float32r)
        self.v_odd = own("v_odd", [P, SLOTS, INNER])
        self.v_even = own("v_even", [P, SLOTS, INNER])
        self.kT = own("kT", [P, PAIRS, WINDOW + K_SLOTS * P])
        self.qT = own("qT", [P, PAIRS, P])
        self.squares = own("squares", [P, 2 * INNER])
        self.norm2 = own("norm2", [P, 2 * HEADS])
        self.inv_norm = own("inv_norm", [P, 2 * HEADS])
        self.rope_a = own("rope_a", [P, 2 * INNER])
        self.rope_b = own("rope_b", [P, 2 * INNER])
        self.roped = own("roped", [P, 2 * INNER])
        self.neg_max = own("neg_max", [P, HEADS])
        self.row_sum = own("row_sum", [P, HEADS])
        self.inv_sum = own("inv_sum", [P, HEADS])
        self.probs = own("probs", [P, HEADS, P])
        self.pT = own("pT", [P, HEADS, P])
        self.oT = own("oT", [P, PAIRS, P])
        self.shifted = own("shifted", [P, TILES, D])
        self.stats = own("stats", [P, GROUP, 6])
        self.mean_var = own("mean_var", [P, 2, GROUP, 2])
        self.var_eps = own("var_eps", [P, 2, GROUP])
        self.rstd = own("rstd", [P, 2, GROUP])
        self.g_kT = self.v_odd[:, 0:2, :].rearrange("p a b -> p (a b)")
        self.g_v = self.v_odd[:, 2:4, :].rearrange("p a b -> p (a b)").rearrange("p (t d) -> p t d", d=D)
        self.g_qT = self.v_even[:, 0:2, :].rearrange("p a b -> p (a b)")
        self.g_probs = [self.probs, self.rope_a[:, :].rearrange("p (a b) -> p a b", b=P)]
        self.g_pT = [self.pT, self.rope_b[:, :].rearrange("p (a b) -> p a b", b=P)]
        self.g_max = own("g_max", [P, 2, 2])
        self.g_negmax = own("g_negmax", [P, 2])
        self.g_sum = own("g_sum", [P, 2, 2])
        self.g_total = own("g_total", [P, 2])
        self.g_inv = own("g_inv", [P, 2])

    def add_semaphores(self, sem):
        def own(name):
            return sem(f"{name}{self.s}")

        self.x_loaded = own("x_loaded")
        self.hT_hi_ready = own("hT_hi_ready")
        self.hT_lo_ready = own("hT_lo_ready")
        self.squares_ready = own("squares_ready")
        self.norm2_ready = own("norm2_ready")
        self.norm2_clipped = own("norm2_clipped")
        self.inv_norm_ready = own("inv_norm_ready")
        self.products_ready = own("products_ready")
        self.rope_sum_ready = own("rope_sum_ready")
        self.roped_ready = own("roped_ready")
        self.qT_ready = own("qT_ready")
        self.kT_ready = own("kT_ready")
        self.v_ready = own("v_ready")
        self.v_shifted = [own(f"v_shifted{i}_") for i in range(SLOTS)]
        self.max_ready = own("max_ready")
        self.exp_ready = own("exp_ready")
        self.inv_sum_ready = own("inv_sum_ready")
        self.probs_ready = own("probs_ready")
        self.pT_ready = own("pT_ready")
        self.oT_ready = own("oT_ready")
        self.attended = own("attended")
        self.y_shifted = own("y_shifted")
        self.stats_ready = own("stats_ready")
        self.mean_var_ready = own("mean_var_ready")
        self.eps_added = own("eps_added")
        self.rstd_ready = own("rstd_ready")
        self.normed_ready = own("normed_ready")
        self.ff_added = own("ff_added")
        self.x_updated = own("x_updated")
        self.gqkv_ready = own("gqkv_ready")
        self.gmax_part = own("gmax_part")
        self.gmax_ready = own("gmax_ready")
        self.gexp_ready = own("gexp_ready")
        self.gtotal_ready = own("gtotal_ready")
        self.ginv_ready = own("ginv_ready")
        self.gpT_ready = own("gpT_ready")
        self.g_added = own("g_added")
        self.stored = own("stored")


def build(nc, x_in, out, w):
    fp32, fp32r, bf16 = mybir.dt.float32, mybir.dt.float32r, mybir.dt.bfloat16
    ALU, ACT, AX = mybir.AluOpType, mybir.ActivationFunctionType, mybir.AxisListType
    ORDER = stage_order()

    fills = [(what, s, m) for stage, s, m in ORDER for what in stage_banks(stage, m)]
    fill = {f: k for k, f in enumerate(fills)}

    ctx = ExitStack()
    with ctx:
        def sb(name, shape, dt=fp32):
            return ctx.enter_context(nc.sbuf_tensor(name, shape, dt))

        first_sem = []

        def sem(name):
            s = ctx.enter_context(nc.semaphore(name))
            first_sem.append(s)
            return s

        wqkv_hi = sb("wqkv_hi", [P, LAYERS, 3 * INNER], fp32r)
        wqkv_lo = sb("wqkv_lo", [P, LAYERS, 3 * INNER], fp32r)
        wo = sb("wo", [P, LAYERS, PAIRS, D])
        w1_hi = sb("w1_hi", [P, LAYERS, W1_COLS], fp32r)
        w1_lo = sb("w1_lo", [P, LAYERS, W1_COLS], fp32r)
        w2 = sb("w2", [P, LAYERS, N_CHUNKS, D])
        b1 = sb("b1", [P, LAYERS, 2, N_CHUNKS])
        ln_g = sb("ln_g", [P, LAYERS])
        ln_b = sb("ln_b", [P, LAYERS])
        gw = sb("gw", [P, 3 * D])
        ident = sb("ident", [P, P])
        ident16 = sb("ident16", [P, P], bf16)
        mask16 = sb("mask16", [P, 3 * P], bf16)
        window_mask = mask16[:, 0:P].unsqueeze(1).to_broadcast([P, PAIRS, P])
        first_mask = mask16[:, P:2 * P].unsqueeze(1).to_broadcast([P, PAIRS, P])
        causal_mask = mask16[:, 2 * P:3 * P]
        cos_t = sb("cos_t", [P, LAYERS, TILES, 2, HEAD_D])
        sin_t = sb("sin_t", [P, LAYERS, TILES, 2, HEAD_D])
        minus_half = sb("minus_half", [P, 2 * HEADS])
        zero_col = sb("zero_col", [P, 1])

        normed = sb("normed", [P, GROUP, D])
        nT = sb("nT", [P, GROUP * P])
        nT_hi = sb("nT_hi", [P, GROUP * P], fp32r)
        nT_lo = sb("nT_lo", [P, GROUP * P], fp32r)
        gate = sb("gate", [P, 2, GROUP * P])
        hid = sb("hid", [P, N_CHUNKS, GROUP * P])
        seqs = [Sequence(sb, s) for s in range(PAIR)]
        q0, q1 = seqs
        wqkv_raw = [v[:, :, :].rearrange("p a b -> p (a b)")[:, 0:3 * INNER] for v in (q1.v_odd, q1.v_even)]
        w1_raw = [v[:, 0:W1_COLS] for v in (q1.rope_a, q1.rope_b)]
        cos_raw = q0.v_odd[:, 0:2, :].rearrange("p a b -> p (a b)").rearrange("p (t j d) -> p t j d", t=TILES, j=2)
        sin_raw = q0.v_odd[:, 2:4, :].rearrange("p a b -> p (a b)").rearrange("p (t j d) -> p t j d", t=TILES, j=2)
        mask_f = q0.v_even[:, :, :].rearrange("p a b -> p (a b)")[:, 0:3 * P]
        qk_gain = q0.squares[:, 0:LAYERS * 4 * HEAD_D].rearrange("p (l a b d) -> p l a b d", l=LAYERS, a=2, b=2)

        banks = [ctx.enter_context(nc.psum_tensor(f"bank{i}", [P, 512], fp32)) for i in range(BANKS)]

        loaded = sem("loaded")
        masks_loaded = sem("masks_loaded")
        tables_loaded = sem("tables_loaded")
        wqkv_loaded = [sem(f"wqkv{lay}_loaded") for lay in range(LAYERS)]
        w1_loaded = sem("w1_loaded")
        set_up = sem("set_up")
        rounded = sem("rounded")
        zeroed = sem("zeroed")
        seq_done = sem("seq_done")
        seq_idle = sem("seq_idle")
        seq_go = sem("seq_go")
        cleared_from = len(first_sem)

        full = [sem(f"full{b}") for b in range(BANKS)]
        nT_ready = sem("nT_ready")
        nT_lo_ready = sem("nT_lo_ready")
        gate_ready = sem("gate_ready")
        hid_ready = sem("hid_ready")
        for q in seqs:
            q.add_semaphores(sem)
        cleared = [s.num for s in first_sem[cleared_from:]]
        assert cleared == list(range(cleared[0], cleared[0] + len(cleared)))

        def pass_of(n):
            return n // (LAYERS * TILES)

        def layer_of(n):
            return n // TILES % LAYERS

        ln_no, through_no, ff_no = {}, {}, {}
        for stage, s, m in ORDER:
            if stage in ("input_stats", "ff_stats", "global_stats"):
                ln_no[stage, s, m] = sum(key[1] == s for key in ln_no)
            if stage in ("ff_norm", "global_norm"):
                through_no[stage, s, m] = len(through_no)
            if stage == "ff_up":
                ff_no[s, m] = len(ff_no)
        ff_stages = [(stage, s, m) for stage, s, m in ORDER if stage in ("ff_up", "ff_down")]
        assert all(up[1:] == down[1:] for up, down in zip(ff_stages[::2], ff_stages[1::2]))
        g_unit = {}
        for t in range(TILES):
            for c in range(t // GROUP + 1):
                g_unit[t, c] = len(g_unit) + 1

        def read_by(what, s, m):
            q = seqs[s]
            c = int(what[-1]) if what[-1].isdigit() else 0
            kind = what.rstrip("0123456789")
            if kind in ("gate", "lin"):
                return (gate_ready if kind == "gate" else hid_ready, N_CHUNKS * ff_no[s, m] + c + 1)
            if kind in ("Gs", "Gp"):
                return (q.gexp_ready if kind == "Gs" else q.gpT_ready, g_unit[m, c])
            if kind in ("ffT", "GxT"):
                return nT_ready, through_no["ff_norm" if kind == "ffT" else "global_norm", s, m] + 1
            return {
                "xT": (q.hT_lo_ready, 2 * m + 2),
                "q": (q.products_ready, 6 * m + 3),
                "k": (q.products_ready, 6 * m + 6),
                "v": (q.v_ready, m + 1),
                "qT": (q.qT_ready, m + 1),
                "kT": (q.kT_ready, m + 1),
                "s": (q.exp_ready, 2 * m + c + 1),
                "p": (q.pT_ready, 2 * m + c + 1),
                "oT": (q.oT_ready, m + 1),
                "y": (q.attended, m + 1),
                "ff": (q.ff_added, m + 1),
                "Gq": (q.gqkv_ready, 3 * m + 1),
                "Gk": (q.gqkv_ready, 3 * m + 2),
                "Gv": (q.gqkv_ready, 3 * m + 3),
                "Go": (q.g_added, m + 1),
            }[kind]

        def bank(what, q, m):
            return banks[fill[what, q.s, m] % BANKS]

        def take_bank(pe, what, q, m):
            k = fill[what, q.s, m]
            if k >= BANKS:
                pe.wait_ge(*read_by(*fills[k - BANKS]))
            return banks[k % BANKS]

        def filled(ins, what, q, m):
            ins.then_inc(full[fill[what, q.s, m] % BANKS], 1)

        def wait_full(eng, what, q, m):
            k = fill[what, q.s, m]
            eng.wait_ge(full[k % BANKS], k // BANKS + 1)
            return banks[k % BANKS]

        def end_sequence(eng, it):
            eng.sem_inc(seq_done, 1)
            eng.wait_ge(seq_go, it + 1)

        block = ctx.enter_context(nc.Block())

        @block.sync
        def _(sp):
            for dst, src, signal in ((ident[:, :], w["ident"], masks_loaded), (mask_f[:, :], w["masks"], masks_loaded),
                                     (wqkv_raw[0], w["wqkv"][:, 0, :], wqkv_loaded[0]),
                                     (cos_raw[:, :, :, :], w["cos"], tables_loaded),
                                     (sin_raw[:, :, :, :], w["sin"], tables_loaded),
                                     (qk_gain[:, :, :, :, :], w["qk_gain"], tables_loaded),
                                     (wqkv_raw[1], w["wqkv"][:, 1, :], wqkv_loaded[1]),
                                     (w1_raw[0], w["w1"][:, 0, :], w1_loaded), (w1_raw[1], w["w1"][:, 1, :], w1_loaded)):
                sp.dma_start(dst, src).then_inc(signal, 16)

            with sp.Fori(0, SEQS // PAIR) as it:
                for q in seqs:
                    sp.dma_start(q.x[:, :, :], x_in[bass.ds(PAIR * it + q.s, 1), :, :].rearrange("s (t p) d -> p (s t) d", p=P)).then_inc(q.x_loaded, 16)
                for stage, s, m in ORDER:
                    q = seqs[s]
                    if stage == "project":
                        slot, slot_before = m % SLOTS, (m - 1) % SLOTS
                        sp.wait_ge(q.v_ready, m + 1)
                        if m >= SLOTS:
                            wait_full(sp, "oT", q, m - SLOTS)
                        if m % TILES > 0:
                            sp.dma_start(q.v_even[0:64, slot, :], q.v_odd[64:128, slot_before, :]).then_inc(q.v_shifted[slot], 16)
                        sp.dma_start(q.v_even[64:128, slot, :], q.v_odd[0:64, slot, :]).then_inc(q.v_shifted[slot], 16)
                    if stage == "ff_shift":
                        g = m % GROUPS
                        a = GROUP * g
                        sp.wait_ge(q.attended, GROUP * (m + 1))
                        up = q.shifted[:, :, 64:128]
                        src = q.y[:, :, 64:128]
                        sp.dma_start(q.shifted[:, a:a + GROUP, 0:64], q.y[:, a:a + GROUP, 0:64]).then_inc(q.y_shifted, 16)
                        sp.dma_start(up[16:128, a:a + GROUP, :], src[15:127, a:a + GROUP, :]).then_inc(q.y_shifted, 16)
                        sp.dma_start(up[1:16, a:a + GROUP, :], src[0:15, a:a + GROUP, :]).then_inc(q.y_shifted, 16)
                        last = min(GROUP, TILES - 1 - a)
                        sp.dma_start(up[0:1, a + 1:a + 1 + last, :], src[127:128, a:a + last, :]).then_inc(q.y_shifted, 16)
                    if stage == "pass_out" and m >= GROUPS:
                        g = m % GROUPS
                        sp.wait_ge(q.x_updated, m + 1)
                        sp.dma_start(out[bass.ds(PAIR * it + s, 1), g * 512:(g + 1) * 512, :].rearrange("s (t p) d -> p (s t) d", p=P),
                                     q.x[:, g * GROUP:(g + 1) * GROUP, :]).then_inc(q.stored, 16)
                for q in seqs:
                    sp.wait_ge(q.stored, 16 * GROUPS)
                sp.wait_ge(seq_done, 4 * it + 4)
                sp.sem_inc(seq_idle, 1)
                sp.sem_clear(range(cleared[0], cleared[-1] + 1))
                sp.sem_inc(seq_go, 1)

        @block.tensor
        def _(pe):
            pe.wait_ge(masks_loaded, 32)
            pe.wait_ge(loaded, 16 * LOADS)
            pe.wait_ge(zeroed, ZEROED)
            pe.wait_ge(set_up, SET_UP)
            with pe.Fori(0, SEQS // PAIR) as it:
                for stage, s, m in ORDER:
                    q = seqs[s]
                    t = m % TILES
                    lay = layer_of(m)
                    if stage == "transpose_x":
                        if lay == 0:
                            pe.wait_ge(q.normed_ready, ln_no["input_stats", s, pass_of(m) * GROUPS + t // GROUP] + 1)
                        else:
                            pe.wait_ge(q.ff_added, m // GROUP - GROUPS + 1)
                        b = take_bank(pe, "xT", q, m)
                        filled(pe.transpose(b[:, 0:P], q.y[:, t, :], ident[:, :]), "xT", q, m)
                    if stage == "project":
                        pe.wait_ge(q.hT_hi_ready, 2 * m + 2)
                        pe.wait_ge(q.hT_lo_ready, 2 * m + 2)
                        cols = slice(m % K_SLOTS * P, (m % K_SLOTS + 1) * P)
                        for j, what in enumerate("qkv"):
                            b = take_bank(pe, what, q, m)
                            out_cols = slice(j * INNER, (j + 1) * INNER)
                            pe.matmul(b[:, :], q.hT_hi[:, cols], wqkv_lo[:, lay, out_cols], start=True, stop=False)
                            pe.matmul(b[:, :], q.hT_lo[:, cols], wqkv_hi[:, lay, out_cols], start=False, stop=False)
                            mm = pe.matmul(b[:, :], q.hT_hi[:, cols], wqkv_hi[:, lay, out_cols], start=False, stop=True)
                            filled(mm, what, q, m)
                    if stage == "transpose_qk":
                        pe.wait_ge(q.roped_ready, m + 1)
                        for j, what in enumerate(("qT", "kT")):
                            b = take_bank(pe, what, q, m)
                            for c in range(PAIRS):
                                mm = pe.transpose(b[:, c * P:(c + 1) * P],
                                                  q.roped[:, j * INNER + c * P:j * INNER + (c + 1) * P], ident[:, :])
                            filled(mm, what, q, m)
                    if stage == "scores":
                        pe.wait_ge(q.qT_ready, m + 1)
                        pe.wait_ge(q.kT_ready, m + 1)
                        for h in range(2):
                            b = take_bank(pe, f"s{h}", q, m)
                            pe.matmul(b[:, :].rearrange("p (c k) -> p c k", c=PAIRS), ident16[:, :],
                                      first_mask if t == 0 else window_mask, start=True, stop=True, skip_group_check=True)
                            r = slice(64 * h, 64 * h + 64)
                            for c in range(PAIRS):
                                for win in range(2):
                                    k0 = m % K_SLOTS * P + win * WINDOW
                                    mm = pe.matmul(b[64 * win:64 * win + 64, c * P:(c + 1) * P], q.qT[r, c, win * 64:win * 64 + 64],
                                                   q.kT[r, c, k0:k0 + 2 * WINDOW], start=False, stop=True,
                                                   skip_group_check=True)
                            filled(mm, f"s{h}", q, m)
                    if stage == "transpose_probs":
                        pe.wait_ge(q.probs_ready, m + 1)
                        for h in range(2):
                            b = take_bank(pe, f"p{h}", q, m)
                            for c in range(PAIRS):
                                mm = pe.transpose(b[:, c * P:(c + 1) * P], q.probs[:, h * PAIRS + c, :], ident[:, :])
                            filled(mm, f"p{h}", q, m)
                    if stage == "mix_values":
                        b = take_bank(pe, "oT", q, m)
                        pe.wait_ge(q.pT_ready, 2 * m + 2)
                        same = [i for i in range(m + 1) if i % SLOTS == m % SLOTS]
                        pe.wait_ge(q.v_shifted[m % SLOTS], sum(32 if i % TILES else 16 for i in same))
                        for win, v in enumerate((q.v_even, q.v_odd)):
                            for c in range(PAIRS):
                                for h in range(2):
                                    head = 2 * c + h
                                    mm = pe.matmul(b[64 * h:64 * h + 64, c * P + win * 64:c * P + win * 64 + 64],
                                                   v[:, m % SLOTS, head * 64:head * 64 + 64],
                                                   q.pT[:, h * PAIRS + c, 64 * win:64 * win + 64],
                                                   start=True, stop=True, skip_group_check=True)
                        filled(mm, "oT", q, m)
                    if stage == "attend_out":
                        pe.wait_ge(q.oT_ready, m + 1)
                        b = take_bank(pe, "y", q, m)
                        for c in range(PAIRS):
                            mm = pe.matmul(b[:, 0:D], q.oT[:, c, :], wo[:, lay, c, :],
                                           start=(c == 0), stop=(c == PAIRS - 1))
                        filled(mm, "y", q, m)
                    if stage in ("ff_up", "ff_down"):
                        lay = m // GROUPS % LAYERS
                    if stage == "ff_transpose":
                        pe.wait_ge(q.normed_ready, ln_no["ff_stats", s, m] + 1)
                        b = take_bank(pe, "ffT", q, m)
                        for i in range(GROUP):
                            mm = pe.transpose(b[:, i * P:(i + 1) * P], normed[:, i, :], ident[:, :])
                        filled(mm, "ffT", q, m)
                    if stage == "ff_up":
                        pe.wait_ge(nT_ready, through_no["ff_norm", s, m] + 1)
                        pe.wait_ge(nT_lo_ready, ff_no[s, m] + 1)
                        for c, (at, size) in enumerate(HID_CHUNKS):
                            for what, base in ((f"gate{c}", HID), (f"lin{c}", 0)):
                                b = take_bank(pe, what, q, m)
                                cols = slice(base + at, base + at + P)
                                pe.matmul(b[:, :], w1_lo[:, lay, cols], nT_hi[:, :], start=True, stop=False)
                                pe.matmul(b[:, :], w1_hi[:, lay, cols], nT_lo[:, :], start=False, stop=False)
                                mm = pe.matmul(b[:, :], w1_hi[:, lay, cols], nT_hi[:, :], start=False, stop=True)
                                filled(mm, what, q, m)
                    if stage == "ff_down":
                        pe.wait_ge(hid_ready, N_CHUNKS * (ff_no[s, m] + 1))
                        b = take_bank(pe, "ff", q, m)
                        for i in range(GROUP):
                            for c, (at, size) in enumerate(HID_CHUNKS):
                                rows = size + 1 if c == N_CHUNKS - 1 else size
                                mm = pe.matmul(b[:, i * P:(i + 1) * P], hid[0:rows, c, i * P:(i + 1) * P],
                                               w2[0:rows, lay, c, :], start=(c == 0), stop=(c == N_CHUNKS - 1))
                        filled(mm, "ff", q, m)
                    if stage == "global_transpose":
                        pe.wait_ge(q.normed_ready, ln_no["global_stats", s, m] + 1)
                        b = take_bank(pe, "GxT", q, m)
                        for i in range(GROUP):
                            mm = pe.transpose(b[:, i * P:(i + 1) * P], normed[:, i, :], ident[:, :])
                        filled(mm, "GxT", q, m)
                    if stage == "global_project":
                        pe.wait_ge(nT_ready, through_no["global_norm", s, m] + 1)
                        for j, what in enumerate(("Gq", "Gk")):
                            b = take_bank(pe, what, q, m)
                            filled(pe.matmul(b[:, :], gw[:, j * D:(j + 1) * D], nT[:, :], start=True, stop=True), what, q, m)
                        b = take_bank(pe, "Gv", q, m)
                        for i in range(GROUP):
                            mm = pe.matmul(b[:, i * P:(i + 1) * P], nT[:, i * P:(i + 1) * P], gw[:, 2 * D:3 * D],
                                           start=True, stop=True)
                        filled(mm, "Gv", q, m)
                    if stage == "global_scores":
                        pe.wait_ge(q.gqkv_ready, 3 * (m // GROUP + 1))
                        for c in range(m // GROUP + 1):
                            b = take_bank(pe, f"Gs{c}", q, m)
                            keys = min((c + 1) * 512, (m + 1) * P) - c * 512
                            diagonal = c == m // GROUP
                            mm = pe.matmul(b[:, 0:keys], q.g_qT[:, m * P:(m + 1) * P], q.g_kT[:, c * 512:c * 512 + keys],
                                           start=True, stop=True)
                            if diagonal:
                                mm = pe.matmul(b[:, keys - P:keys], ident16[:, :], causal_mask, start=False, stop=True,
                                               skip_group_check=True)
                            filled(mm, f"Gs{c}", q, m)
                    if stage == "global_probs":
                        for c in range(m // GROUP + 1):
                            pe.wait_ge(q.gexp_ready, g_unit[m, c])
                            b = take_bank(pe, f"Gp{c}", q, m)
                            for j in range(min(GROUP, m + 1 - c * GROUP)):
                                mm = pe.transpose(b[:, j * P:(j + 1) * P], q.g_probs[m % 2][:, c * GROUP + j, :], ident[:, :])
                            filled(mm, f"Gp{c}", q, m)
                    if stage == "global_mix":
                        b = take_bank(pe, "Go", q, m)
                        for j in range(m + 1):
                            if j % GROUP == 0:
                                pe.wait_ge(q.gpT_ready, g_unit[m, j // GROUP])
                            mm = pe.matmul(b[:, 0:D], q.g_pT[m % 2][:, j, :], q.g_v[:, j, :], start=(j == 0), stop=(j == m))
                        filled(mm, "Go", q, m)
                end_sequence(pe, it)

        @block.scalar
        def _(act):
            for lay in range(LAYERS):
                act.wait_ge(wqkv_loaded[lay], 16)
                act.activation(wqkv_hi[:, lay, :], wqkv_raw[lay], ACT.Copy).then_inc(rounded, 1)
            act.wait_ge(w1_loaded, 32)
            for lay in range(LAYERS):
                act.activation(w1_hi[:, lay, :], w1_raw[lay], ACT.Copy).then_inc(rounded, 1)
            for dst, src in ((wo[:, :, :, :], w["wo"]), (w2[:, :, :, :], w["w2"]), (b1[:, :, :, :], w["b1"]),
                             (ln_g[:, :], w["ln_g"]), (ln_b[:, :], w["ln_b"]), (gw[:, :], w["gw"])):
                act.dma_start(dst, src).then_inc(loaded, 16)
            act.wait_ge(loaded, 16 * LOADS)
            act.wait_ge(zeroed, ZEROED)
            act.wait_ge(set_up, SET_UP)

            with act.Fori(0, SEQS // PAIR) as it:
                for stage, s, m in ORDER:
                    q = seqs[s]
                    t = m % TILES
                    lay = layer_of(m)
                    if stage == "transpose_x":
                        b = wait_full(act, "xT", q, m)
                        at = m % K_SLOTS * P
                        act.activation(q.hT_hi[0:64, at:at + P], b[0:64, 0:P], ACT.Copy).then_inc(q.hT_hi_ready, 1)
                        ins = act.activation(q.hT_hi[64:128, at + 1:at + P + 1], b[64:128, 0:P], ACT.Copy)
                        if m % K_SLOTS == K_SLOTS - 1:
                            before = b[64:128, P - 1:P] if t < TILES - 1 else zero_col[64:128, :]
                            ins = act.activation(q.hT_hi[64:128, 0:1], before, ACT.Copy)
                        ins.then_inc(q.hT_hi_ready, 1)
                    if stage == "project":
                        if m:
                            act.wait_ge(q.norm2_ready, m)
                        for j, what in enumerate("qk"):
                            b = wait_full(act, what, q, m)
                            ins = act.activation(q.squares[:, j * INNER:(j + 1) * INNER], b[:, :], ACT.Square)
                            ins.then_inc(q.squares_ready, 1)
                        b = wait_full(act, "v", q, m)
                        ins = act.activation(q.v_odd[:, m % SLOTS, :], b[:, :], ACT.Copy)
                        ins.then_inc(q.v_ready, 1)
                    if stage == "transpose_qk":
                        b = wait_full(act, "qT", q, m)
                        ins = act.activation(q.qT[:, :, :], b[:, :].rearrange("p (c q) -> p c q", c=PAIRS), ACT.Copy)
                        ins.then_inc(q.qT_ready, 1)
                        b = wait_full(act, "kT", q, m)
                        kT_new = b[:, :].rearrange("p (c k) -> p c k", c=PAIRS)
                        at = WINDOW + m % K_SLOTS * P
                        ins = act.activation(q.kT[:, :, at:at + P], kT_new, ACT.Copy)
                        if m % K_SLOTS == K_SLOTS - 1:
                            ins = act.activation(q.kT[:, :, 0:WINDOW], kT_new[:, :, WINDOW:P], ACT.Copy)
                        ins.then_inc(q.kT_ready, 1)
                    if stage == "scores":
                        for h in range(2):
                            act.wait_ge(q.max_ready, 2 * m + h + 1)
                            b = bank(f"s{h}", q, m)
                            for c in range(PAIRS):
                                i = h * PAIRS + c
                                ins = act.activation(q.probs[:, i, :], b[:, c * P:(c + 1) * P], ACT.Exp,
                                                     bias=q.neg_max[:, i:i + 1], scale=1.0,
                                                     accum_out=q.row_sum[:, i:i + 1])
                            ins.then_inc(q.exp_ready, 1)
                    if stage == "transpose_probs":
                        for h in range(2):
                            b = wait_full(act, f"p{h}", q, m)
                            act.activation(q.pT[:, h * PAIRS:(h + 1) * PAIRS, :].rearrange("p c r -> p (c r)"), b[:, :],
                                           ACT.Copy).then_inc(q.pT_ready, 1)
                    if stage in ("ff_transpose", "ff_up"):
                        lay = m // GROUPS % LAYERS
                    if stage == "ff_transpose":
                        b = wait_full(act, "ffT", q, m)
                        act.activation(nT_hi[:, :], b[:, :], ACT.Identity, bias=ln_b[:, lay:lay + 1], scale=ln_g[:, lay:lay + 1])
                        ins = act.activation(nT[:, :], b[:, :], ACT.Identity, bias=ln_b[:, lay:lay + 1], scale=ln_g[:, lay:lay + 1])
                        ins.then_inc(nT_ready, 1)
                    if stage == "ff_up":
                        for c, (at, size) in enumerate(HID_CHUNKS):
                            b = wait_full(act, f"gate{c}", q, m)
                            k = N_CHUNKS * ff_no[s, m] + c
                            if k >= 2:
                                act.wait_ge(hid_ready, k - 1)
                            ins = act.activation(gate[0:size, k % 2, :], b[0:size, :], ACT.Gelu, bias=b1[0:size, lay, 1, c:c + 1])
                            ins.then_inc(gate_ready, 1)
                    if stage == "global_transpose":
                        b = wait_full(act, "GxT", q, m)
                        ins = act.activation(nT[:, :], b[:, :], ACT.Copy)
                        ins.then_inc(nT_ready, 1)
                    if stage == "global_project":
                        a = m * GROUP
                        for what, dst in (("Gq", q.g_qT[:, a * P:a * P + 512]), ("Gk", q.g_kT[:, a * P:a * P + 512]),
                                          ("Gv", q.g_v[:, a:a + GROUP, :].rearrange("p t d -> p (t d)"))):
                            b = wait_full(act, what, q, m)
                            ins = act.activation(dst, b[:, :], ACT.Copy)
                            ins.then_inc(q.gqkv_ready, 1)
                    if stage == "global_scores":
                        act.wait_ge(q.gmax_ready, m + 1)
                        for c in range(m // GROUP + 1):
                            b = bank(f"Gs{c}", q, m)
                            keys = min((c + 1) * 512, (m + 1) * P) - c * 512
                            ins = act.activation(q.g_probs[m % 2][:, c * GROUP:c * GROUP + keys // P, :].rearrange("p a b -> p (a b)"),
                                                 b[:, 0:keys], ACT.Exp, bias=q.g_negmax[:, m % 2:m % 2 + 1], scale=SCORE_SCALE,
                                                 accum_out=q.g_sum[:, m % 2, c:c + 1])
                            ins.then_inc(q.gexp_ready, 1)
                end_sequence(act, it)

        @block.vector
        def _(dve):
            dve.wait_ge(masks_loaded, 32)
            dve.tensor_copy(ident16[:, :], ident[:, :]).then_inc(set_up, 1)
            dve.tensor_copy(mask16[:, :], mask_f[:, :]).then_inc(set_up, 1)

            def split_rest(lo, raw, hi, step):
                dve.wait_ge(rounded, step)
                dve.tensor_tensor(lo, raw, hi.bitcast(fp32), ALU.subtract).then_inc(set_up, 1)

            split_rest(wqkv_lo[:, 0, :], wqkv_raw[0], wqkv_hi[:, 0, :], 1)
            dve.wait_ge(tables_loaded, 48)
            for lay in range(LAYERS):
                for raw, table, j in ((cos_raw, cos_t, 0), (sin_raw, sin_t, 1)):
                    for i in range(2):
                        gain = qk_gain[:, lay, j, i, :].unsqueeze(1).to_broadcast([P, TILES, HEAD_D])
                        dve.tensor_tensor(table[:, lay, :, i, :], raw[:, :, i, :], gain, ALU.mult).then_inc(set_up, 1)
            split_rest(wqkv_lo[:, 1, :], wqkv_raw[1], wqkv_hi[:, 1, :], 2)
            for lay in range(LAYERS):
                split_rest(w1_lo[:, lay, :], w1_raw[lay], w1_hi[:, lay, :], LAYERS + lay + 1)
            dve.wait_ge(loaded, 16 * LOADS)
            dve.wait_ge(set_up, SET_UP)
            dve.wait_ge(zeroed, ZEROED)

            def token_stats(q, unit, src):
                if unit:
                    dve.wait_ge(q.mean_var_ready, GROUP * unit)
                for i in range(GROUP):
                    dve.bn_stats(q.stats[:, i, :], src[:, i, :]).then_inc(q.stats_ready, 1)
                dve.wait_ge(q.stats_ready, GROUP * (unit + 1))
                for i in range(GROUP):
                    dve.bn_aggr(q.mean_var[:, unit % 2, i, :], q.stats[:, i, :]).then_inc(q.mean_var_ready, 1)

            def normalise(q, unit, src, dst):
                dve.wait_ge(q.rstd_ready, unit + 1)
                for i in range(GROUP):
                    ins = dve.tensor_scalar(dst[:, i, :], src[:, i, :], q.mean_var[:, unit % 2, i, 0:1], q.rstd[:, unit % 2, i:i + 1],
                                            ALU.subtract, ALU.mult)
                ins.then_inc(q.normed_ready, 1)

            with dve.Fori(0, SEQS // PAIR) as it:
                for stage, s, m in ORDER:
                    q = seqs[s]
                    t = m % TILES
                    lay = layer_of(m)
                    a = m % GROUPS * GROUP
                    if stage == "input_stats":
                        if m == 0:
                            dve.wait_ge(q.x_loaded, 16)
                        if m >= GROUPS:
                            dve.wait_ge(q.g_added, a + GROUP)
                        token_stats(q, ln_no[stage, s, m], q.x[:, a:a + GROUP, :])
                    if stage == "input_norm":
                        normalise(q, ln_no["input_stats", s, m], q.x[:, a:a + GROUP, :], q.y[:, a:a + GROUP, :])
                    if stage == "transpose_x":
                        b = bank("xT", q, m)
                        at = m % K_SLOTS * P
                        dve.wait_ge(q.hT_hi_ready, 2 * m + 2)
                        dve.tensor_tensor(q.hT_lo[0:64, at:at + P], b[0:64, 0:P], q.hT_hi[0:64, at:at + P].bitcast(fp32),
                                          ALU.subtract).then_inc(q.hT_lo_ready, 1)
                        if m % K_SLOTS == K_SLOTS - 1:
                            before = b[64:128, P - 1:P] if t < TILES - 1 else zero_col[64:128, :]
                            dve.tensor_tensor(q.hT_lo[64:128, 0:1], before, q.hT_hi[64:128, 0:1].bitcast(fp32), ALU.subtract)
                        ins = dve.tensor_tensor(q.hT_lo[64:128, at + 1:at + P + 1], b[64:128, 0:P],
                                                q.hT_hi[64:128, at + 1:at + P + 1].bitcast(fp32), ALU.subtract)
                        ins.then_inc(q.hT_lo_ready, 1)
                    if stage == "project":
                        if m:
                            dve.wait_ge(q.roped_ready, m)
                        for j, what in enumerate("qk"):
                            dve.wait_ge(q.squares_ready, 2 * m + j + 1)
                            b = bank(what, q, m)
                            a_out = q.rope_a[:, j * INNER:(j + 1) * INNER]
                            b_out = q.rope_b[:, j * INNER:(j + 1) * INNER]
                            cos = cos_t[:, lay, t, j, :].unsqueeze(1).to_broadcast([P, HEADS, HEAD_D])
                            dve.tensor_tensor(a_out.rearrange("p (h d) -> p h d", h=HEADS),
                                              b[:, :].rearrange("p (h d) -> p h d", h=HEADS), cos, ALU.mult).then_inc(q.products_ready, 1)
                            for half in range(2):
                                o, i = half * HALF, (1 - half) * HALF
                                sin = sin_t[:, lay, t, j, o:o + HALF].unsqueeze(1).to_broadcast([P, HEADS, HALF])
                                ins = dve.tensor_tensor(b_out.rearrange("p (h d) -> p h d", h=HEADS)[:, :, o:o + HALF],
                                                        b[:, :].rearrange("p (h d) -> p h d", h=HEADS)[:, :, i:i + HALF],
                                                        sin, ALU.mult)
                                ins.then_inc(q.products_ready, 1)
                    if stage == "norm_sums":
                        if m:
                            dve.wait_ge(q.inv_norm_ready, m)
                        dve.tensor_reduce(q.norm2[:, :], q.squares[:, :].rearrange("p (h d) -> p h d", d=HEAD_D),
                                          AX.X, ALU.add).then_inc(q.norm2_ready, 1)
                        dve.wait_ge(q.norm2_ready, m + 1)
                        dve.tensor_scalar(q.norm2[:, :], q.norm2[:, :], NORM2_MIN, None, ALU.max).then_inc(q.norm2_clipped, 1)
                    if stage == "rope_finish":
                        dve.wait_ge(q.rope_sum_ready, m + 1)
                        dve.wait_ge(q.inv_norm_ready, m + 1)
                        if m:
                            wait_full(dve, "kT", q, m - 1)
                        inv = q.inv_norm[:, :].unsqueeze(2).to_broadcast([P, 2 * HEADS, HEAD_D])
                        dve.tensor_tensor(q.roped[:, :].rearrange("p (h d) -> p h d", d=HEAD_D),
                                          q.rope_a[:, :].rearrange("p (h d) -> p h d", d=HEAD_D), inv,
                                          ALU.mult).then_inc(q.roped_ready, 1)
                    if stage == "scores":
                        for h in range(2):
                            b = wait_full(dve, f"s{h}", q, m)
                            dve.tensor_reduce(q.neg_max[:, h * PAIRS:(h + 1) * PAIRS],
                                              b[:, :].rearrange("p (c k) -> p c k", c=PAIRS), AX.X, ALU.max,
                                              negate=True).then_inc(q.max_ready, 1)
                    if stage == "probs_finish":
                        dve.wait_ge(q.exp_ready, 2 * m + 2)
                        dve.reciprocal(q.inv_sum[:, :], q.row_sum[:, :]).then_inc(q.inv_sum_ready, 1)
                    if stage == "mix_values":
                        b = wait_full(dve, "oT", q, m)
                        ins = dve.tensor_copy(q.oT[:, :, :], b[:, :].rearrange("p (c q) -> p c q", c=PAIRS))
                        ins.then_inc(q.oT_ready, 1)
                    if stage == "attend_out":
                        b = wait_full(dve, "y", q, m)
                        ins = dve.tensor_tensor(q.y[:, t, :], b[:, 0:D], q.y[:, t, :], ALU.add)
                        ins.then_inc(q.attended, 1)
                    if stage == "ff_stats":
                        dve.wait_ge(q.y_shifted, 4 * 16 * (m + 1))
                        token_stats(q, ln_no[stage, s, m], q.shifted[:, a:a + GROUP, :])
                    if stage in ("ff_norm", "global_norm"):
                        if through_no[stage, s, m]:
                            dve.wait_ge(nT_ready, through_no[stage, s, m])
                    if stage == "ff_norm":
                        normalise(q, ln_no["ff_stats", s, m], q.shifted[:, a:a + GROUP, :], normed[:, :, :])
                    if stage == "ff_transpose":
                        dve.wait_ge(nT_ready, through_no["ff_norm", s, m] + 1)
                        dve.tensor_tensor(nT_lo[:, :], nT[:, :], nT_hi[:, :].bitcast(fp32), ALU.subtract).then_inc(nT_lo_ready, 1)
                    if stage == "ff_up":
                        lay = m // GROUPS % LAYERS
                        for c, (at, size) in enumerate(HID_CHUNKS):
                            b = wait_full(dve, f"lin{c}", q, m)
                            k = N_CHUNKS * ff_no[s, m] + c
                            dve.wait_ge(gate_ready, k + 1)
                            ins = dve.scalar_tensor_tensor(hid[0:size, c, :], b[0:size, :], b1[0:size, lay, 0, c:c + 1],
                                                           gate[0:size, k % 2, :], ALU.add, ALU.mult)
                            ins.then_inc(hid_ready, 1)
                    if stage == "ff_down":
                        a = m % GROUPS * GROUP
                        b = wait_full(dve, "ff", q, m)
                        rows = q.y[:, a:a + GROUP, :].rearrange("p t d -> p (t d)")
                        ins = dve.tensor_tensor(rows, b[:, :], rows, ALU.add)
                        ins.then_inc(q.ff_added, 1)
                    if stage == "pass_out":
                        g = m % GROUPS
                        i = m // GROUPS
                        dve.wait_ge(q.ff_added, (i * LAYERS + LAYERS - 1) * GROUPS + g + 1)
                        rows = slice(g * GROUP, (g + 1) * GROUP)
                        dve.scalar_tensor_tensor(q.x[:, rows, :].rearrange("p t d -> p (t d)"),
                                                 q.y[:, rows, :].rearrange("p t d -> p (t d)"), 0.5,
                                                 q.x[:, rows, :].rearrange("p t d -> p (t d)"),
                                                 ALU.mult, ALU.add).then_inc(q.x_updated, 1)
                    if stage == "global_stats":
                        dve.wait_ge(q.x_updated, m + 1)
                        token_stats(q, ln_no[stage, s, m], q.x[:, a:a + GROUP, :])
                    if stage == "global_norm":
                        normalise(q, ln_no["global_stats", s, m], q.x[:, a:a + GROUP, :], normed[:, :, :])
                    if stage == "global_scores":
                        for c in range(m // GROUP + 1):
                            b = wait_full(dve, f"Gs{c}", q, m)
                            keys = min((c + 1) * 512, (m + 1) * P) - c * 512
                            dve.tensor_reduce(q.g_max[:, m % 2, c:c + 1], b[:, 0:keys], AX.X, ALU.max).then_inc(q.gmax_part, 1)
                        dve.wait_ge(q.gmax_part, g_unit[m, m // GROUP])
                        if m < GROUP:
                            ins = dve.tensor_scalar(q.g_negmax[:, m % 2:m % 2 + 1], q.g_max[:, m % 2, 0:1], -SCORE_SCALE, None, ALU.mult)
                        else:
                            ins = dve.tensor_scalar(q.g_negmax[:, m % 2:m % 2 + 1], q.g_max[:, m % 2, 0:1],
                                                    q.g_max[:, m % 2, 1:2], -SCORE_SCALE, ALU.max, ALU.mult)
                        ins.then_inc(q.gmax_ready, 1)
                    if stage == "global_probs":
                        for c in range(m // GROUP + 1):
                            b = wait_full(dve, f"Gp{c}", q, m)
                            tiles = min(GROUP, m + 1 - c * GROUP)
                            ins = dve.tensor_copy(q.g_pT[m % 2][:, c * GROUP:c * GROUP + tiles, :].rearrange("p a b -> p (a b)"),
                                                  b[:, 0:tiles * P])
                            ins.then_inc(q.gpT_ready, 1)
                        dve.wait_ge(q.gexp_ready, g_unit[m, m // GROUP])
                        total = q.g_sum[:, m % 2, 0:1]
                        if m >= GROUP:
                            total = q.g_total[:, m % 2:m % 2 + 1]
                            dve.tensor_tensor(total, q.g_sum[:, m % 2, 0:1], q.g_sum[:, m % 2, 1:2], ALU.add).then_inc(q.gtotal_ready, 1)
                            dve.wait_ge(q.gtotal_ready, m - GROUP + 1)
                        if m >= 2:
                            dve.wait_ge(q.g_added, m - 1)
                        dve.reciprocal(q.g_inv[:, m % 2:m % 2 + 1], total).then_inc(q.ginv_ready, 1)
                    if stage == "global_mix":
                        b = wait_full(dve, "Go", q, m)
                        dve.wait_ge(q.ginv_ready, m + 1)
                        ins = dve.scalar_tensor_tensor(q.x[:, m, :], b[:, 0:D], q.g_inv[:, m % 2:m % 2 + 1], q.x[:, m, :],
                                                       ALU.mult, ALU.add)
                        ins.then_inc(q.g_added, 1)
                end_sequence(dve, it)

        @block.gpsimd
        def _(pool):
            parts = [(hid[64:128, N_CHUNKS - 1, :], 1.0),
                     (minus_half[:, :], -0.5), (zero_col[:, :], 0.0)]
            for q in seqs:
                parts += [(q.hT_hi[64:128, 0:1].bitcast(fp32), 0.0),
                          (q.hT_lo[64:128, 0:1].bitcast(fp32), 0.0),
                          (q.kT[:, :, 0:WINDOW], 0.0),
                          (q.shifted[0:1, 0, 64:128], 0.0)]
            parts += [(q.v_even[0:64, 0, :], 0.0) for q in seqs]
            assert len(parts) == ZEROED
            for i, (part, value) in enumerate(parts):
                if i == ZEROED - PAIR:
                    pool.wait_ge(set_up, SET_UP)
                if i:
                    pool.wait_ge(zeroed, i)
                pool.memset(part, value).then_inc(zeroed, 1)
            pool.wait_ge(zeroed, ZEROED)
            with pool.Fori(0, SEQS // PAIR) as it:
                for stage, s, m in ORDER:
                    q = seqs[s]
                    if stage == "project":
                        pool.wait_ge(q.products_ready, 6 * (m + 1))
                        pool.tensor_tensor(q.rope_a[:, :], q.rope_a[:, :], q.rope_b[:, :], ALU.add).then_inc(q.rope_sum_ready, 1)
                    if stage == "norm_sums":
                        pool.wait_ge(q.norm2_clipped, m + 1)
                        if m:
                            pool.wait_ge(q.roped_ready, m)
                        pool.tensor_tensor(q.inv_norm[:, :], q.norm2[:, :], minus_half[:, :], ALU.pow).then_inc(q.inv_norm_ready, 1)
                    if stage == "probs_finish":
                        pool.wait_ge(q.inv_sum_ready, m + 1)
                        inv = q.inv_sum[:, :].unsqueeze(2).to_broadcast([P, HEADS, P])
                        pool.tensor_tensor(q.probs[:, :, :], q.probs[:, :, :], inv, ALU.mult).then_inc(q.probs_ready, 1)
                    if (stage, s, m) in ln_no:
                        u = ln_no[stage, s, m]
                        pool.wait_ge(q.mean_var_ready, GROUP * (u + 1))
                        pool.tensor_scalar(q.var_eps[:, u % 2, :], q.mean_var[:, u % 2, :, 1], LN_EPS, None, ALU.add).then_inc(q.eps_added, 1)
                        pool.wait_ge(q.eps_added, u + 1)
                        if u >= 2:
                            pool.wait_ge(q.normed_ready, u - 1)
                        pool.tensor_tensor(q.rstd[:, u % 2, :], q.var_eps[:, u % 2, :], minus_half[:, 0:GROUP], ALU.pow).then_inc(q.rstd_ready, 1)
                end_sequence(pool, it)


def kernel(L0_attn_x, L0_attn_W_qkv, L0_ffn_wqkv, L0_ffn_q_scale, L0_ffn_k_scale, L0_ffn_wo, L0_ffn_ln_g,
           L0_ffn_ln_b, L0_ffn_w1, L0_ffn_b1, L0_ffn_w2, L0_ffn_b2):
    import concourse.bacc as bacc
    from concourse.bass_utils import run_bass_kernel_spmd

    f = np.float32
    half_idx = np.arange(0, HEAD_D, 2, dtype=f)
    inv_freq = (f(1.0) / f(10000.0) ** (half_idx / f(HEAD_D))).astype(f)
    pos = np.arange(N_TOK, dtype=f)
    angle = pos[:, None] * inv_freq[None, :]
    base = ((half_idx + f(0.4 * HEAD_D)) / f(1.4 * HEAD_D)).astype(f)
    xpos = base[None, :] ** ((pos - N_TOK // 2) / f(WINDOW // 2))[:, None]
    angle, xpos = (np.concatenate([a, a], axis=1) for a in (angle, xpos))
    sign = np.where(np.arange(HEAD_D) < HALF, f(-1), f(1))
    qk_scale = f(8.0)
    cos = np.stack([qk_scale * np.cos(angle) * xpos, np.cos(angle) / xpos], axis=1)
    sin = np.stack([qk_scale * np.sin(angle) * xpos * sign, np.sin(angle) / xpos * sign], axis=1)
    cos, sin = (np.ascontiguousarray(a.reshape(TILES, P, 2, HEAD_D).transpose(1, 0, 2, 3).astype(f)) for a in (cos, sin))
    i, j = np.arange(P)[:, None] % WINDOW, np.arange(P)[None, :]
    inside = (j >= i) & (j <= i + WINDOW)
    window = np.where(inside, f(0), f(MASKED))
    first_window = (np.arange(P)[:, None] < WINDOW) & (j < WINDOW)
    first = np.where(inside & ~first_window, f(0), f(MASKED))
    causal = np.where(j <= np.arange(P)[:, None], f(0), f(MASKED))
    masks = np.concatenate([window, first, causal], axis=1).astype(f)

    def swap(a):
        return np.concatenate([a[:, HALF:], a[:, :HALF]], axis=1)

    qs, ks = np.asarray(L0_ffn_q_scale), np.asarray(L0_ffn_k_scale)
    gain = np.stack([np.stack([qs, ks], axis=1), np.stack([swap(qs), swap(ks)], axis=1)], axis=1)
    b1 = np.asarray(L0_ffn_b1)
    w1_cols = np.zeros((P, LAYERS, W1_COLS), f)
    w1_cols[:, :, :2 * HID] = np.asarray(L0_ffn_w1).transpose(1, 0, 2)
    b1_cols = np.zeros((P, LAYERS, 2, N_CHUNKS), f)
    w2 = np.asarray(L0_ffn_w2)
    w2_rows = np.zeros((P, LAYERS, N_CHUNKS, D), f)
    for c, (at, size) in enumerate(HID_CHUNKS):
        for part in range(2):
            b1_cols[:size, :, part, c] = b1[:, part * HID + at:part * HID + at + size].T
        w2_rows[:size, :, c, :] = w2[:, at:at + size, :].transpose(1, 0, 2)
    w2_rows[B2_ROW, :, N_CHUNKS - 1, :] = np.asarray(L0_ffn_b2)
    arrays = {
        "x": np.asarray(L0_attn_x),
        "wqkv": np.asarray(L0_ffn_wqkv).transpose(1, 0, 2),
        "wo": np.asarray(L0_ffn_wo).reshape(LAYERS, PAIRS, P, D).transpose(2, 0, 1, 3),
        "w1": w1_cols,
        "w2": w2_rows, "b1": b1_cols,
        "ln_g": np.asarray(L0_ffn_ln_g).T, "ln_b": np.asarray(L0_ffn_ln_b).T,
        "gw": np.asarray(L0_attn_W_qkv),
        "qk_gain": np.broadcast_to(gain[None], (P,) + gain.shape),
        "ident": np.eye(P, dtype=f), "masks": masks, "cos": cos, "sin": sin,
    }
    arrays = {k: np.ascontiguousarray(a) for k, a in arrays.items()}
    nc = bacc.Bacc("TRN2", target_bir_lowering=False, num_devices=1)
    aps = {k: nc.dram_tensor(f"in_{k}", a.shape, mybir.dt.float32, kind="ExternalInput").ap() for k, a in arrays.items()}
    out = nc.dram_tensor("out_x", (SEQS, N_TOK, D), mybir.dt.float32, kind="ExternalOutput").ap()
    build(nc, aps["x"], out, aps)
    r = run_bass_kernel_spmd(nc, [{f"in_{k}": a for k, a in arrays.items()}], core_ids=[0])
    return r.results[0]["out_x"]
```
